# Optimizing a Trainium2 kernel written in Bass

```python
import numpy as np
import jax
import jax.numpy as jnp

def _softmax(x, axis=-1):
    return jax.nn.softmax(x, axis=axis)

def _gelu(x):
    return jax.nn.gelu(x, approximate=True)

def _silu(x):
    return jax.nn.silu(x)

def _sigmoid(x):
    return jax.nn.sigmoid(x)

def _layernorm(x, axis=-1, eps=1e-05):
    m = jnp.mean(x, axis=axis, keepdims=True)
    v = jnp.var(x, axis=axis, keepdims=True)
    return (x - m) / jnp.sqrt(v + eps)

def _scatter_add(tgt, idx, src, axis=0):
    return tgt.at[idx].add(src)

def _segment_sum(src, seg, n):
    return jax.ops.segment_sum(src, seg, n)
kernel_name = 'mk_gps_d1_gnn_r8_9a852e'

def setup_inputs(seed: int=0):
    np.random.seed(seed)
    _w = jnp.asarray

    def _rec_inputs():
        import jax
        import jax.numpy as jnp
        _gk = jax.random.key(seed)
        x = -8.776e-05 + 1 * jax.random.normal(jax.random.fold_in(_gk, 1), (6250, 512), jnp.float32)
        src = jax.random.randint(jax.random.fold_in(_gk, 2), (100000,), 0, 6250, jnp.int32)
        dst = jnp.minimum((6250 * jax.random.uniform(jax.random.fold_in(_gk, 3), (100000,)) ** 2.0).astype(jnp.int32), 49999)
        _o = jnp.argsort(dst, stable=True)
        src = src[_o]
        dst = dst[_o]
        return (x, src, dst)
    x, src, dst = _rec_inputs()

    def _L0_gnn_setup():
        import jax, jax.numpy as jnp
        import numpy as np
        N_NODES = 1250
        N_EDGES = 20000
        IN_DIM = 512
        OUT_DIM = 512
        LN_EPS = 1e-05
        key = jax.random.key(seed)
        k_x, k_src, k_ws, k_wn = jax.random.split(key, 4)
        x = jax.random.normal(k_x, (N_NODES, IN_DIM), dtype=jnp.float32)
        edge_src = jax.random.randint(k_src, (N_EDGES,), 0, N_NODES, dtype=jnp.int32)
        edge_dst = jnp.repeat(jnp.arange(N_NODES, dtype=jnp.int32), N_EDGES // N_NODES)
        deg = jnp.full((N_NODES,), float(N_EDGES // N_NODES), dtype=jnp.float32)
        scale = 1.0 / np.sqrt(IN_DIM)
        W_self = jax.random.normal(k_ws, (OUT_DIM, IN_DIM), dtype=jnp.float32) * scale
        W_neigh = jax.random.normal(k_wn, (OUT_DIM, IN_DIM), dtype=jnp.float32) * scale
        bias = jnp.zeros((OUT_DIM,), dtype=jnp.float32)
        gamma = jnp.ones((OUT_DIM,), dtype=jnp.float32)
        beta = jnp.zeros((OUT_DIM,), dtype=jnp.float32)
        return {'x': x, 'edge_src': edge_src, 'edge_dst': edge_dst, 'deg': deg, 'W_self': W_self, 'W_neigh': W_neigh, 'bias': bias, 'gamma': gamma, 'beta': beta}
    _L0_gnn_all = _L0_gnn_setup()
    _L0_gnn_in = {k: v for k, v in _L0_gnn_all.items() if k in ('W_self', 'W_neigh', 'bias', 'gamma', 'beta')}
    del _L0_gnn_all

    def _L0_mix_setup():
        import jax, jax.numpy as jnp
        import numpy as np
        HEADS = 8
        DIM_HEAD = 64
        EPS = 1e-05

        def layer_norm(x, gamma):
            mu = jnp.mean(x, axis=-1, keepdims=True)
            var = jnp.var(x, axis=-1, keepdims=True)
            return (x - mu) * jax.lax.rsqrt(var + EPS) * gamma
        key = jax.random.key(seed)
        k1, k2, k3 = jax.random.split(key, 3)
        b, n, dim = (4, 2048, 512)
        hidden = HEADS * DIM_HEAD
        x = jax.random.normal(k1, (b, n, dim), dtype=jnp.float32)
        norm_gamma = jnp.ones((dim,), dtype=jnp.float32)
        w_qkv = jax.random.normal(k2, (hidden * 3, dim), dtype=jnp.float32) * dim ** (-0.5)
        w_out = jax.random.normal(k3, (dim, hidden), dtype=jnp.float32) * hidden ** (-0.5)
        out_gamma = jnp.ones((dim,), dtype=jnp.float32)
        return {'x': x, 'norm_gamma': norm_gamma, 'w_qkv': w_qkv, 'w_out': w_out, 'out_gamma': out_gamma}
    _L0_mix_all = _L0_mix_setup()
    _L0_mix_in = {k: v for k, v in _L0_mix_all.items() if k in ('norm_gamma', 'w_qkv', 'w_out', 'out_gamma')}
    del _L0_mix_all

    def _L0_ffn_setup():
        import jax, jax.numpy as jnp
        import numpy as np
        B, S, D, H, E = (4, 1024, 512, 256, 8)
        key = jax.random.key(seed)
        ks = jax.random.split(key, 7)
        scale = 1.0 / np.sqrt(D)
        return {'x': jax.random.normal(ks[0], (B, S, D), dtype=jnp.float32), 'Wg': jax.random.normal(ks[1], (D, E), dtype=jnp.float32) * scale, 'bg': jnp.zeros((E,), dtype=jnp.float32), 'W1': jax.random.normal(ks[2], (E, D, H), dtype=jnp.float32) * scale, 'b1': jnp.zeros((E, H), dtype=jnp.float32), 'W2': jax.random.normal(ks[3], (E, H, D), dtype=jnp.float32) * (1.0 / np.sqrt(H)), 'b2': jnp.zeros((E, D), dtype=jnp.float32)}
    _L0_ffn_all = _L0_ffn_setup()
    _L0_ffn_in = {k: v for k, v in _L0_ffn_all.items() if k in ('Wg', 'bg', 'W1', 'b1', 'W2', 'b2')}
    del _L0_ffn_all
    return {'x': x, 'src': src, 'dst': dst, 'L0_gnn_W_self': _L0_gnn_in['W_self'], 'L0_gnn_W_neigh': _L0_gnn_in['W_neigh'], 'L0_gnn_bias': _L0_gnn_in['bias'], 'L0_gnn_gamma': _L0_gnn_in['gamma'], 'L0_gnn_beta': _L0_gnn_in['beta'], 'L0_mix_norm_gamma': _L0_mix_in['norm_gamma'], 'L0_mix_w_qkv': _L0_mix_in['w_qkv'], 'L0_mix_w_out': _L0_mix_in['w_out'], 'L0_mix_out_gamma': _L0_mix_in['out_gamma'], 'L0_ffn_Wg': _L0_ffn_in['Wg'], 'L0_ffn_bg': _L0_ffn_in['bg'], 'L0_ffn_W1': _L0_ffn_in['W1'], 'L0_ffn_b1': _L0_ffn_in['b1'], 'L0_ffn_W2': _L0_ffn_in['W2'], 'L0_ffn_b2': _L0_ffn_in['b2']}

def reference(x, src, dst, L0_gnn_W_self, L0_gnn_W_neigh, L0_gnn_bias, L0_gnn_gamma, L0_gnn_beta, L0_mix_norm_gamma, L0_mix_w_qkv, L0_mix_w_out, L0_mix_out_gamma, L0_ffn_Wg, L0_ffn_bg, L0_ffn_W1, L0_ffn_b1, L0_ffn_W2, L0_ffn_b2):
    import jax
    import jax.numpy as jnp

    def _L0_gnn_ref(x, edge_src, edge_dst, deg, W_self, W_neigh, bias, gamma, beta):
        import jax, jax.numpy as jnp
        import numpy as np
        N_NODES = 1250
        N_EDGES = 20000
        IN_DIM = 512
        OUT_DIM = 512
        LN_EPS = 1e-05
        n = x.shape[0]
        h_self = jnp.einsum('nd,od->no', x, W_self)
        neigh_sum = jax.ops.segment_sum(x[edge_src], edge_dst, num_segments=n)
        neigh_mean = neigh_sum / jnp.maximum(deg, 1.0)[:, None]
        h_neigh = jnp.einsum('nd,od->no', neigh_mean, W_neigh)
        h = h_self + h_neigh + bias
        mu = jnp.mean(h, axis=-1, keepdims=True)
        var = jnp.mean(jnp.square(h - mu), axis=-1, keepdims=True)
        h = (h - mu) * jax.lax.rsqrt(var + LN_EPS)
        return h * gamma + beta

    def _L0_mix_ref(x, norm_gamma, w_qkv, w_out, out_gamma):
        import jax, jax.numpy as jnp
        import numpy as np
        HEADS = 8
        DIM_HEAD = 64
        EPS = 1e-05

        def layer_norm(x, gamma):
            mu = jnp.mean(x, axis=-1, keepdims=True)
            var = jnp.var(x, axis=-1, keepdims=True)
            return (x - mu) * jax.lax.rsqrt(var + EPS) * gamma
        b, n, dim = x.shape
        h, d = (HEADS, DIM_HEAD)
        scale = d ** (-0.5)
        x = layer_norm(x, norm_gamma)
        qkv = jnp.einsum('bnc,fc->bnf', x, w_qkv)
        q, k, v = jnp.split(qkv, 3, axis=-1)
        to_bhnd = lambda t: t.reshape(b, n, h, d).transpose(0, 2, 1, 3)
        q, k, v = (to_bhnd(q), to_bhnd(k), to_bhnd(v))
        q = jax.nn.softmax(q, axis=-1) * scale
        k = jax.nn.softmax(k, axis=-2)
        context = jnp.einsum('bhnd,bhne->bhde', k, v)
        out = jnp.einsum('bhde,bhnd->bhne', context, q)
        out = out.transpose(0, 2, 1, 3).reshape(b, n, h * d)
        out = jnp.einsum('bnf,cf->bnc', out, w_out)
        return layer_norm(out, out_gamma)

    def _L0_ffn_ref(x, Wg, bg, W1, b1, W2, b2):
        import jax, jax.numpy as jnp
        import numpy as np
        B, S, D, H, E = (4, 1024, 512, 256, 8)
        b, s, d = x.shape
        xf = x.reshape(-1, d)
        logits = xf @ Wg + bg
        scores = jax.nn.softmax(logits, axis=-1)
        top_s, top_i = jax.lax.top_k(scores, 1)
        idx = top_i[:, 0]
        sc = top_s[:, 0]
        n_experts = Wg.shape[1]
        out = jnp.zeros_like(xf)
        for e in range(n_experts):
            h = jax.nn.relu(xf @ W1[e] + b1[e]) @ W2[e] + b2[e]
            out = jnp.where((idx == e)[:, None], h, out)
        out = out * sc[:, None]
        return out.reshape(b, s, d)
    deg = jnp.maximum(jax.ops.segment_sum(jnp.ones(dst.shape, jnp.float32), dst, num_segments=6250), 1.0)
    xn = _layernorm(x, axis=-1)
    x = x + _L0_gnn_ref(xn, src, dst, deg, L0_gnn_W_self, L0_gnn_W_neigh, L0_gnn_bias, L0_gnn_gamma, L0_gnn_beta) + _L0_mix_ref(xn[None], L0_mix_norm_gamma, L0_mix_w_qkv, L0_mix_w_out, L0_mix_out_gamma)[0]
    x = x + _L0_ffn_ref(_layernorm(x, axis=-1)[None], L0_ffn_Wg, L0_ffn_bg, L0_ffn_W1, L0_ffn_b1, L0_ffn_W2, L0_ffn_b2)[0]
    return x

_drawn_inputs = setup_inputs


def setup_inputs(seed=0):
    import zlib

    import numpy as np

    out = dict(_drawn_inputs(seed))
    spreads = {'L0_gnn_bias': (0.0, 0.1),
     'L0_gnn_gamma': (1.0, 0.2),
     'L0_gnn_beta': (0.0, 0.1),
     'L0_mix_norm_gamma': (1.0, 0.2),
     'L0_mix_out_gamma': (1.0, 0.2),
     'L0_ffn_bg': (0.0, 0.1),
     'L0_ffn_b1': (0.0, 0.527),
     'L0_ffn_b2': (0.0, 0.364)}
    factors = {}
    for name, (base, spread) in spreads.items():
        noise = np.random.default_rng([zlib.crc32(name.encode()), seed]).standard_normal(out[name].shape)
        drawn = base * np.exp(spread * noise) if base else spread * noise
        out[name] = jnp.asarray(drawn.astype(out[name].dtype))
    for name, factor in factors.items():
        out[name] = (out[name] * factor).astype(out[name].dtype)
    return out
```

```python
from contextlib import ExitStack

import numpy as np

import concourse.bass as bass
import concourse.mybir as mybir

F32, F16, I32, I16 = mybir.dt.float32, mybir.dt.float16, mybir.dt.int32, mybir.dt.int16
ALU = mybir.AluOpType
ACT = mybir.ActivationFunctionType
AX = mybir.AxisListType
MAX_ALL = bass.bass_isa.ReduceOp.max

P = 128
N_NODES, DIM = 6250, 512
N_EDGES = 100000
HEADS, HEAD_DIM = 8, 64
PAIRS = HEADS // 2
EXPERTS, HIDDEN = 8, 256
EPS = 1e-5
TILES = -(-N_NODES // P)
ROWS = TILES * P
CHUNK = 7
CHUNKS = TILES // CHUNK
KC = DIM // P
GROUP = 2
GROUPS = -(-N_EDGES // (GROUP * P)) + 1
G_PART = 98
G_BLOCKS = GROUPS // G_PART
ENTRIES = 441
EDGE_COLS = GROUP * (GROUPS + 1)
PER_CHUNK = ENTRIES // CHUNKS
PER_STEP = 8
RING = 7
AHEAD = 3
XS = 2048.0
BIG = 1e30
X1W = 528
BUCKET = ROWS
XT = ROWS // P + EXPERTS - 1
UNROLL = 8
ROUNDS = 44

assert CHUNKS * CHUNK == TILES and G_PART * G_BLOCKS == GROUPS and PER_CHUNK * CHUNKS == ENTRIES
assert GROUPS + TILES - 1 <= ENTRIES


class Names:
    pass


class Memory:

    def __init__(self, nc, ctx, stage):
        self.nc, self.ctx, self.stage, self.named = nc, ctx, stage, []
        ctx.callback(self.clear)

    def clear(self):
        if self.named:
            self.nc.clear_and_free_semaphores(self.named)
            self.nc.all_engine_barrier()

    def sb(self, name, shape, dtype=F32):
        return self.ctx.enter_context(self.nc.sbuf_tensor(f"{self.stage}_{name}", shape, dtype))

    def ps(self, name, shape, dtype=F32):
        return self.ctx.enter_context(self.nc.psum_tensor(f"{self.stage}_{name}", shape, dtype))

    def sem(self, name):
        self.named.append(self.nc.alloc_semaphore(name=f"{self.stage}_{name}"))
        return self.named[-1]

    def sems(self, name, n):
        return [self.sem(f"{name}{i}") for i in range(n)]


def flat(ap):
    return ap.rearrange("p a b -> p (a b)")


def bcast(ap, n):
    return ap.unsqueeze(2).to_broadcast([ap.shape[0], ap.shape[1], n])


def wait_past(eng, sem, count):
    if not (isinstance(count, int) and count <= 0):
        eng.wait_ge(sem, count)


def chunks(eng, body):
    body(0)
    with eng.Fori(1, CHUNKS) as c:
        body(c)


def in_turn(eng, total, unroll, lag, body):
    for t in range(unroll):
        body(t, t)
    with eng.Fori(1, total // unroll) as c:
        for i in range(unroll):
            body(unroll * c + i, i)
    for t in range(total, total + lag):
        body(t, t % unroll)


def stage(total, t, lag):
    at = t - lag
    return at if not isinstance(t, int) or 0 <= at < total else None


def count_before(t, i):
    return t if i == 0 else t - 1


class Chain:

    def __init__(self, eng, sem, n, t):
        self.eng, self.sem, self.n, self.t, self.k = eng, sem, n, t, 0

    def __call__(self, ins):
        self.k += 1
        assert self.k <= self.n
        ins.then_inc(self.sem, 1)
        self.eng.wait_ge(self.sem, self.n * self.t + self.k)


def power_of_two(dve, link, out, biggest, one_over, tmp_i):
    link(dve.tensor_scalar(out, biggest, 1e-30, None, ALU.max))
    link(dve.tensor_scalar(tmp_i, out.bitcast(I32), 0x7F800000, None, ALU.bitwise_and))
    link(dve.tensor_scalar(one_over, tmp_i.bitcast(F32), 2.0 ** -14, None, ALU.mult))
    link(dve.reciprocal(out, one_over))


def entry_groups(dve, link, K, begun, holds):
    for b in range(G_BLOCKS):
        link(dve.tensor_scalar(begun[:, :], K.pos[0:G_PART, 0:ENTRIES], K.gstart[:, b:b + 1], None, ALU.is_ge))
        ins = dve.scalar_tensor_tensor(out=holds[:, b, :], in0=K.pos[0:G_PART, 0:ENTRIES], scalar=K.gend[:, b:b + 1],
                                       in1=begun[:, :], op0=ALU.is_lt, op1=ALU.mult)
        if b < G_BLOCKS - 1:
            link(ins)
    return ins


def entry_sums(pe, K, psum_e, holds):
    for r in range(3):
        for b in range(G_BLOCKS):
            mm = pe.matmul(psum_e[r][:, 0:ENTRIES], K.lhs[:, r, b:b + 1], holds[:, b, :],
                           start=(b == 0), stop=(b == G_BLOCKS - 1))
    return mm


def entry_values(dve, link, K, psum_e, wrow):
    link(dve.tensor_scalar(K.ent[:, 0, 0:ENTRIES], psum_e[0][:, 0:ENTRIES], float(GROUPS), float(GROUP), ALU.add, ALU.mult))
    link(dve.tensor_tensor(wrow[:, :], psum_e[2][:, 0:ENTRIES], K.pos[0:1, 0:ENTRIES], ALU.mult))
    link(dve.tensor_tensor(K.ent[:, 1, 0:ENTRIES], psum_e[1][:, 0:ENTRIES], wrow[:, :], ALU.add))


def normalize(nc, K, D):
    with ExitStack() as ctx:
        m = Memory(nc, ctx, "normalize")
        x = m.sb("x", [P, CHUNK, DIM])
        xn = m.sb("xn", [P, CHUNK, DIM])
        halves = m.sb("halves", [P, CHUNK, 2, DIM], F16)
        stats = m.sb("stats", [P, CHUNK, 6])
        mv = m.sb("mv", [P, CHUNK, 2])
        sd = m.sb("sd", [P, CHUNK])
        veps = m.sb("veps", [P, CHUNK])
        scale = m.sb("scale", [P, CHUNK])
        shift = m.sb("shift", [P, CHUNK])
        var_all = m.sb("var_all", [P, TILES])
        inv_all = m.sb("inv_all", [P, TILES])
        sd_all = m.sb("sd_all", [P, TILES])
        staged = 3 * KC
        wq = flat(K.acc[:, 0:staged, :]).rearrange("p (a b) -> p a b", a=KC)
        gam = m.sb("gam", [P, KC])
        wmax = m.sb("wmax", [P, 1])
        wall = m.sb("wall", [P, 1])
        wscale = m.sb("wscale", [P, 1])
        wbits = m.sb("wbits", [P, 1], I32)
        unscale = m.sb("unscale", [P, 1])
        src_i, dst_i = m.sb("src_i", [P, EDGE_COLS], I32), m.sb("dst_i", [P, EDGE_COLS], I32)
        dst_g = m.sb("dst_g", [G_PART, G_BLOCKS, GROUP * P], I32)
        gwin = m.sb("gwin", [G_PART, 2, G_BLOCKS], I32)
        gcount = m.sb("gcount", [G_PART, G_BLOCKS])
        glast = m.sb("glast", [G_PART, G_BLOCKS])
        before = m.sb("before", [G_PART, G_BLOCKS])
        begun = m.sb("begun", [G_PART, ENTRIES])
        holds = m.sb("holds", [G_PART, G_BLOCKS, ENTRIES])
        wrow = m.sb("wrow", [1, ENTRIES])
        oob = m.sb("oob", [P, (EXPERTS * BUCKET + P) // P], I32)
        psum_c = m.ps("psum_c", [P, 512])
        psum_e = [m.ps(f"psum_e{i}", [1, 512]) for i in range(3)]
        x_in, stored = m.sems("x_in", CHUNK), m.sems("stored", CHUNK)
        w_in, e_in, oob_st = m.sem("w_in"), m.sem("e_in"), m.sem("oob_st")
        x_free, stat_ok, mv_ok, veps_ok, sd_ok, inv_ok, scale_ok = (m.sem(s) for s in (
            "x_free", "stat_ok", "mv_ok", "veps_ok", "sd_ok", "inv_ok", "scale_ok"))
        hi_ok, lo_ok = m.sem("hi_ok"), m.sem("lo_ok")
        made, link_ok, wmax_ok, wall_ok = m.sem("made"), m.sem("link_ok"), m.sem("wmax_ok"), m.sem("wall_ok")
        split_ok, spare = m.sem("split_ok"), m.sem("spare")
        cnt_ok, prefix_ok, holds_ok, ent_ok = m.sem("cnt_ok"), m.sem("prefix_ok"), m.sem("holds_ok"), m.sem("ent_ok")
        var2_ok, sd2_ok = m.sem("var2_ok"), m.sem("sd2_ok")
        block = ctx.enter_context(nc.Block())

        @block.sync
        def _(sp):
            for i in range(CHUNK):
                sp.dma_start(x[:, i, :], D["x"][i * P:(i + 1) * P, :]).then_inc(x_in[i], 16)
            sp.dma_start(dst_g[:, :, :], D["dst_groups"]).then_inc(e_in, 16)
            sp.dma_start(dst_i[:, :], D["dst"]).then_inc(e_in, 16)
            sp.dma_start(src_i[:, :], D["src"]).then_inc(e_in, 16)
            sp.dma_start(wq[:, :, :], D["wqkv"]).then_inc(w_in, 16)
            sp.dma_start(gam[:, :], D["norm_gamma"]).then_inc(w_in, 16)

            def store(c, i):
                sp.wait_ge(lo_ok, CHUNK * c + i + 1)
                sp.dma_start(D["table"][bass.ds((CHUNK * c + i) * P, P), :],
                             flat(halves[:, i, :, :])).then_inc(stored[i], 16)

            with sp.Fori(0, CHUNKS - 1) as c:
                for i in range(CHUNK):
                    sp.wait_ge(x_free, CHUNK * c + i + 1)
                    sp.dma_start(x[:, i, :], D["x"][bass.ds((CHUNK * (c + 1) + i) * P, P), :]).then_inc(x_in[i], 16)
                    store(c, i)
            for i in range(CHUNK):
                store(CHUNKS - 1, i)
            sp.wait_ge(made, 8)
            sp.dma_start(D["perm"].rearrange("(p a) b -> p (a b)", p=P), oob[:, :]).then_inc(oob_st, 16)
            for i in range(CHUNK):
                sp.wait_ge(stored[i], 16 * CHUNKS)
            sp.wait_ge(oob_st, 16)

        @block.gpsimd
        def _(pool):
            pool.memset(K.ident[:, :], 0.0).then_inc(made, 1)
            pool.memset(K.upper[:, :], 1.0).then_inc(made, 1)
            pool.memset(K.ones[:, :], 1.0).then_inc(made, 1)
            pool.memset(K.pad_bias[:, :], 0.0).then_inc(made, 1)
            pool.memset(oob[:, :], ROWS).then_inc(made, 1)
            pool.iota(K.pos[:, :], [[1, 512]], base=0, channel_multiplier=0,
                      allow_small_or_imprecise_dtypes=True).then_inc(made, 1)
            pool.iota(K.part[:, :], [[G_PART, G_BLOCKS]], base=-GROUPS, channel_multiplier=1,
                      allow_small_or_imprecise_dtypes=True).then_inc(made, 1)
            pool.iota(K.base[:, :], [[-P, TILES]], base=0, channel_multiplier=0,
                      allow_small_or_imprecise_dtypes=True).then_inc(made, 1)
            pool.wait_ge(made, 8)
            pool.affine_select(out=K.ident[:, :], in_=K.ident[:, :], compare_op=ALU.not_equal, fill=1.0, base=0,
                               pattern=[[-1, P]], channel_multiplier=1).then_inc(made, 1)
            pool.affine_select(out=K.upper[:, :], in_=K.upper[:, :], compare_op=ALU.is_gt, fill=0.0, base=0,
                               pattern=[[1, P]], channel_multiplier=-1).then_inc(made, 1)
            pool.affine_select(out=K.pad_bias[:, :], in_=K.pad_bias[:, :], compare_op=ALU.is_gt, fill=-BIG,
                               base=N_NODES, pattern=[[-P, TILES]], channel_multiplier=-1).then_inc(made, 1)
            pool.iota(K.node[:, :], [[0, 1]], base=0, channel_multiplier=1,
                      allow_small_or_imprecise_dtypes=True).then_inc(made, 1)
            pool.memset(K.deg[:, :], 0.0).then_inc(made, 1)
            pool.memset(K.kmax[:, :], -BIG).then_inc(made, 1)
            pool.memset(K.m_old[:, :], -BIG).then_inc(made, 1)
            pool.memset(K.context[:, :, :], 0.0).then_inc(made, 1)
            pool.wait_ge(wmax_ok, 1)
            pool.partition_all_reduce(wall[:, :], wmax[:, :], P, MAX_ALL).then_inc(wall_ok, 1)
            for t in range(staged, TILES):
                pool.memset(K.acc[:, t, :], 0.0).then_inc(made, 1)
            pool.wait_ge(split_ok, 1)
            for t in range(staged):
                pool.memset(K.acc[:, t, :], 0.0).then_inc(made, 1)

        @block.scalar
        def _(act):
            def tiles(c):
                act.wait_ge(veps_ok, c + 1)
                act.activation(sd[:, :], veps[:, :], ACT.Sqrt).then_inc(sd_ok, 1)
                act.wait_ge(scale_ok, c + 1)
                for i in range(CHUNK):
                    wait_past(act, stored[i], 16 * c)
                    act.activation(xn[:, i, :], x[:, i, :], ACT.Identity, bias=shift[:, i:i + 1],
                                   scale=scale[:, i:i + 1]).then_inc(x_free, 1)
                    act.wait_ge(x_free, CHUNK * c + i + 1)
                    act.copy(halves[:, i, 0, :], xn[:, i, :]).then_inc(hi_ok, 1)

            chunks(act, tiles)
            act.wait_ge(var2_ok, 1)
            act.activation(sd_all[:, :], inv_all[:, :], ACT.Sqrt).then_inc(sd2_ok, 1)

        @block.tensor
        def _(pe):
            pe.wait_ge(made, 11)
            pe.wait_ge(cnt_ok, 1)
            pe.matmul(psum_c[0:G_PART, 0:G_BLOCKS], K.upper[0:G_PART, 0:G_PART], gcount[:, :], start=True, stop=True)
            pe.matmul(psum_c[0:G_PART, G_BLOCKS:2 * G_BLOCKS], K.ones[0:G_PART, 0:G_PART], gcount[:, :],
                      start=True, stop=True).then_inc(prefix_ok, 1)
            pe.wait_ge(holds_ok, 1)
            mm = entry_sums(pe, K, psum_e, holds)
            mm.then_inc(ent_ok, 1)

        @block.vector
        def _(dve):
            done = [0]

            def link(ins):
                done[0] += 1
                ins.then_inc(link_ok, 1)
                dve.wait_ge(link_ok, done[0])

            def edge_tables():
                dve.wait_ge(e_in, 48)
                dve.wait_ge(made, 11)
                link(dve.tensor_copy(K.dst[:, :], dst_i[:, :]))
                link(dve.tensor_copy(K.src[:, :], src_i[:, :]))
                link(dve.memset(K.ent[:, :, :], 0))
                link(dve.tensor_reduce(gwin[:, 0, :], dst_g[:, :, :], AX.X, ALU.min))
                link(dve.tensor_reduce(gwin[:, 1, :], dst_g[:, :, :], AX.X, ALU.max))
                link(dve.tensor_scalar(gwin[:, :, :], gwin[:, :, :], 7, None, ALU.arith_shift_right))
                link(dve.tensor_copy(K.gfirst[:, :], gwin[:, 0, :]))
                link(dve.tensor_copy(glast[:, :], gwin[:, 1, :]))
                link(dve.tensor_tensor(gcount[:, :], glast[:, :], K.gfirst[:, :], ALU.subtract))
                dve.tensor_scalar(gcount[:, :], gcount[:, :], 1.0, None, ALU.add).then_inc(cnt_ok, 1)
                dve.wait_ge(prefix_ok, 1)
                link(dve.memset(before[:, 0:1], 0.0))
                for b in range(1, G_BLOCKS):
                    link(dve.tensor_tensor(before[:, b:b + 1], before[:, b - 1:b],
                                           psum_c[0:G_PART, G_BLOCKS + b - 1:G_BLOCKS + b], ALU.add))
                link(dve.tensor_tensor(K.gstart[:, :], before[:, :], psum_c[0:G_PART, 0:G_BLOCKS], ALU.add))
                link(dve.tensor_tensor(K.gend[:, :], K.gstart[:, :], gcount[:, :], ALU.add))
                link(dve.tensor_copy(K.lhs[:, 0, :], K.part[0:G_PART, :]))
                link(dve.tensor_tensor(K.lhs[:, 1, :], K.gfirst[:, :], K.gstart[:, :], ALU.subtract))
                link(dve.memset(K.lhs[:, 2, :], 1.0))
                ins = entry_groups(dve, link, K, begun, holds)
                ins.then_inc(holds_ok, 1)
                dve.wait_ge(ent_ok, 1)
                entry_values(dve, link, K, psum_e, wrow)
                link(dve.tensor_tensor(before[:, 0:1], before[:, G_BLOCKS - 1:G_BLOCKS],
                                       psum_c[0:G_PART, 2 * G_BLOCKS - 1:2 * G_BLOCKS], ALU.add))
                link(dve.tensor_scalar(wrow[:, 0:ROUNDS], K.pos[0:1, 1:ROUNDS + 1], float(ENTRIES), before[0:1, 0:1],
                                       ALU.mult, ALU.is_lt))
                link(dve.tensor_reduce(glast[0:1, 0:1], wrow[:, 0:ROUNDS], AX.X, ALU.add))
                link(dve.tensor_copy(K.rounds[:, :], glast[0:1, 0:1]))

            def weights_max():
                dve.wait_ge(w_in, 32)
                for k in range(KC):
                    link(dve.tensor_scalar(wq[:, k, :], wq[:, k, :], gam[:, k:k + 1], None, ALU.mult))
                dve.tensor_reduce(wmax[:, :], flat(wq[:, :, :]), AX.X, ALU.max,
                                  apply_absolute_value=True).then_inc(wmax_ok, 1)

            def weights_split():
                dve.wait_ge(wall_ok, 1)
                power_of_two(dve, link, wscale[:, :], wall[:, :], unscale[:, :], wbits[:, :])
                link(dve.tensor_scalar(flat(K.wq_hi[:, :, :]), flat(wq[:, :, :]), wscale[:, :], None, ALU.mult))
                dve.scalar_tensor_tensor(out=flat(K.wq_lo[:, :, :]), in0=flat(wq[:, :, :]), scalar=wscale[:, :],
                                         in1=flat(K.wq_hi[:, :, :]), op0=ALU.mult, op1=ALU.subtract).then_inc(split_ok, 1)

            def tiles(c):
                for i in range(CHUNK):
                    dve.wait_ge(x_in[i], 16 * (c + 1))
                    dve.bn_stats(stats[:, i, :], x[:, i, :]).then_inc(stat_ok, 1)
                dve.wait_ge(stat_ok, CHUNK * (c + 1))
                dve.sem_inc(spare, 1)
                for i in range(CHUNK):
                    dve.bn_aggr(mv[:, i, :], stats[:, i, :]).then_inc(mv_ok, 1)
                dve.wait_ge(mv_ok, CHUNK * (c + 1))
                dve.tensor_scalar(veps[:, :], mv[:, :, 1], EPS, None, ALU.add).then_inc(veps_ok, 1)
                dve.tensor_copy(var_all[:, bass.ds(CHUNK * c, CHUNK)], mv[:, :, 1])
                dve.wait_ge(sd_ok, c + 1)
                dve.reciprocal(inv_all[:, bass.ds(CHUNK * c, CHUNK)], sd[:, :]).then_inc(inv_ok, 1)
                dve.wait_ge(inv_ok, 3 * c + 1)
                wait_past(dve, x_free, CHUNK * c)
                dve.tensor_scalar(scale[:, :], inv_all[:, bass.ds(CHUNK * c, CHUNK)], XS, None,
                                  ALU.mult).then_inc(inv_ok, 1)
                dve.wait_ge(inv_ok, 3 * c + 2)
                dve.tensor_tensor(shift[:, :], mv[:, :, 0], scale[:, :], ALU.mult).then_inc(inv_ok, 1)
                dve.wait_ge(inv_ok, 3 * c + 3)
                dve.tensor_scalar(shift[:, :], shift[:, :], -1.0, None, ALU.mult).then_inc(scale_ok, 1)
                for i in range(CHUNK):
                    dve.wait_ge(hi_ok, CHUNK * c + i + 1)
                    dve.tensor_tensor(halves[:, i, 1, :], xn[:, i, :], halves[:, i, 0, :],
                                      ALU.subtract).then_inc(lo_ok, 1)

            weights_max()
            chunks(dve, tiles)
            edge_tables()
            weights_split()
            link(dve.tensor_copy(K.scratch[:, 0:TILES], inv_all[:, :]))
            link(dve.tensor_tensor(inv_all[:, :], inv_all[:, :], K.scratch[:, 0:TILES], ALU.mult))
            link(dve.tensor_tensor(inv_all[:, :], inv_all[:, :], var_all[:, :], ALU.mult))
            dve.tensor_scalar(inv_all[:, :], inv_all[:, :], EPS, None, ALU.add).then_inc(var2_ok, 1)
            dve.wait_ge(sd2_ok, 1)
            link(dve.reciprocal(K.rq[:, :], sd_all[:, :]))
            link(dve.tensor_scalar(K.rq[:, :], K.rq[:, :], unscale[:, :], 1.0 / XS, ALU.mult, ALU.mult))
            link(dve.tensor_copy(K.ident16[:, :], K.ident[:, :]))
            link(dve.tensor_copy(K.iota16[:, :], K.pos[:, 0:P]))
            link(dve.tensor_copy(K.ones16[:, :], K.ones[:, 0:1]))


def aggregate(nc, K, D):
    with ExitStack() as ctx:
        m = Memory(nc, ctx, "aggregate")
        rows = m.sb("rows", [P, RING, GROUP, 2 * DIM], F16)
        picks = m.sb("picks", [P, RING, GROUP, P], F16)
        cols = m.sb("cols", [P, RING, GROUP], I32)
        xrow = m.sb("xrow", [P, 2 * KC, P], F16)
        x_t = m.sb("x_t", [P, 2 * KC, P], F16)
        q = m.sb("q", [P, HEADS, HEAD_DIM])
        q_exp = m.sb("q_exp", [P, HEADS, HEAD_DIM])
        q_top = m.sb("q_top", [P, HEADS])
        q_sum = m.sb("q_sum", [P, HEADS])
        kbuf = m.sb("kbuf", [P, CHUNK, DIM])
        vbuf = m.sb("vbuf", [P, CHUNK, PAIRS, P + 1])
        rq, pad_bias = m.sb("rq", [P, CHUNK]), m.sb("pad_bias", [P, CHUNK])
        rq_ok = m.sem("rq_ok")
        m_new = m.sb("m_new", [P, PAIRS])
        m_step = m.sb("m_step", [P, PAIRS])
        decay = m.sb("decay", [P, PAIRS])
        diag = flat(q_exp[:, :, :]).rearrange("p (a b) -> p a b", a=PAIRS)
        ag = [m.ps(f"ag{i}", [P, DIM]) for i in range(2)]
        dg = m.ps("dg", [P, 512])
        bank_a, bank_b = m.ps("bank_a", [P, DIM]), m.ps("bank_b", [P, DIM])
        tp = m.ps("tp", [P, 2 * KC, P], F16)
        ct = [m.ps(f"ct{i}", [P, 2, P + 1]) for i in range(2)]
        col_ok, picks_ok, ag_ok, acc_ok, deg_ok = (m.sem(s) for s in (
            "col_ok", "picks_ok", "ag_ok", "acc_ok", "deg_ok"))
        g_in = K.g_in
        spare = m.sem("spare")
        xr_in, tp_ok, xt_ok = m.sem("xr_in"), m.sem("tp_ok"), m.sem("xt_ok")
        q_ok, k_ok, v_ok = m.sem("q_ok"), m.sem("k_ok"), m.sem("v_ok")
        q_sub, q_exp_ok, q_chain, q_done, q_st = (m.sem(s) for s in ("q_sub", "q_exp_ok", "q_chain", "q_done", "q_st"))
        k_in, v_in, kmax_ok = m.sem("k_in"), m.sem("v_in"), m.sem("kmax_ok")
        ones_ok, kt_ok, m_chain, diag_ok, mb_ok = (m.sem(s) for s in ("ones_ok", "kt_ok", "m_chain", "diag_ok", "mb_ok"))
        decay_ok, k_less, k_exp, ct_ok, ct_done = (m.sem(s) for s in ("decay_ok", "k_less", "k_exp", "ct_ok", "ct_done"))
        block = ctx.enter_context(nc.Block())

        @block.sync
        def _(sp):
            def chunk(c):
                for i in range(CHUNK):
                    t = CHUNK * c + i
                    wait_past(sp, tp_ok, t)
                    sp.dma_start(flat(xrow[:, :, :]), D["table"][bass.ds(t * P, P), :]).then_inc(xr_in, 16)
                    if i > 0:
                        sp.wait_ge(q_done, t)
                        sp.dma_start(D["q"][bass.ds((t - 1) * P, P), :], flat(q[:, :, :])).then_inc(q_st, 16)
                sp.wait_ge(q_done, CHUNK * c + CHUNK)
                sp.dma_start(D["q"][bass.ds((CHUNK * c + CHUNK - 1) * P, P), :], flat(q[:, :, :])).then_inc(q_st, 16)

            chunks(sp, chunk)
            sp.wait_ge(q_st, 16 * TILES)

        @block.gpsimd
        def _(pool):
            pool.memset(vbuf[:, :, :, P:P + 1], 1.0).then_inc(ones_ok, 1)

            def chunk(c):
                for e in range(PER_CHUNK):
                    n, slot = PER_CHUNK * c + e, e % RING
                    group = pool.value_load(K.ent[0:1, 0, bass.ds(n, 1)], min_val=0, max_val=EDGE_COLS - GROUP)
                    wait_past(pool, ag_ok, n - RING + 1)
                    pool.tensor_copy(cols[:, slot, :], K.src[:, bass.ds(group, GROUP)]).then_inc(col_ok, 1)
                    pool.wait_ge(col_ok, n + 1)
                    pool.sem_inc(spare, 1)
                    for u in range(GROUP):
                        pool.indirect_dma_start(rows[:, slot, u, :], None, D["table"],
                                                bass.IndirectOffsetOnAxis(ap=cols[:, slot, u:u + 1], axis=0)
                                                ).then_inc(g_in[slot], 16)

            chunks(pool, chunk)

        @block.tensor
        def _(pe):
            def entry(c, e):
                n, slot = PER_CHUNK * c + e, e % RING
                pe.wait_ge(g_in[slot], 16 * GROUP * (PER_CHUNK // RING * c + e // RING + 1))
                pe.wait_ge(picks_ok, n + 1)
                wait_past(pe, acc_ok, n if e == 0 else n - 1)
                for u in range(GROUP):
                    for h in range(2):
                        pe.matmul(ag[e % 2][:, :], picks[:, slot, u, :], rows[:, slot, u, h * DIM:(h + 1) * DIM],
                                  start=(u == 0 and h == 0), stop=(u == GROUP - 1 and h == 1))
                wait_past(pe, deg_ok, n)
                for u in range(GROUP):
                    mm = pe.matmul(dg[:, e % 2:e % 2 + 1], picks[:, slot, u, :], K.ones16[:, :],
                                   start=(u == 0), stop=(u == GROUP - 1))
                mm.then_inc(ag_ok, 1)

            def project(bank, part):
                w = slice(part * DIM, (part + 1) * DIM)
                todo = [(a, b, k) for k in range(KC) for a, b in ((0, K.wq_hi), (0, K.wq_lo), (KC, K.wq_hi))]
                for j, (a, b, k) in enumerate(todo):
                    mm = pe.matmul(bank[:, :], x_t[:, a + k, :], b[:, k, w], start=(j == 0), stop=(j == len(todo) - 1))
                return mm

            def chunk(c):
                for i in range(CHUNK):
                    t, e0 = CHUNK * c + i, PER_STEP * i
                    pe.wait_ge(xr_in, 16 * (t + 1))
                    wait_past(pe, xt_ok, t)
                    for k in range(2 * KC):
                        mm = pe.transpose(tp[:, k, :], xrow[:, k, :], K.ident16[:, :])
                    mm.then_inc(tp_ok, 1)
                    entry(c, e0)
                    entry(c, e0 + 1)
                    pe.wait_ge(xt_ok, t + 1)
                    if i > 0:
                        pe.wait_ge(v_in, t)
                    else:
                        wait_past(pe, v_in, t)
                        wait_past(pe, m_chain, c * 3)
                    project(bank_a, 0).then_inc(q_ok, 1)
                    entry(c, e0 + 2)
                    entry(c, e0 + 3)
                    wait_past(pe, k_in, t)
                    if i == 0:
                        wait_past(pe, k_less, CHUNK * c)
                    project(bank_b, 1).then_inc(k_ok, 1)
                    entry(c, e0 + 4)
                    entry(c, e0 + 5)
                    pe.wait_ge(q_sub, t + 1)
                    project(bank_a, 2).then_inc(v_ok, 1)
                    entry(c, e0 + 6)
                    entry(c, e0 + 7)
                e1 = PER_STEP * CHUNK
                pe.wait_ge(kmax_ok, CHUNK * (c + 1))
                pe.wait_ge(v_in, CHUNK * (c + 1))
                for p in range(PAIRS):
                    mm = pe.transpose(bank_a[:, p * P:(p + 1) * P], K.kmax[:, p * P:(p + 1) * P], K.ident[:, :])
                mm.then_inc(kt_ok, 1)
                entry(c, e1)
                entry(c, e1 + 1)
                pe.wait_ge(diag_ok, c + 1)
                for p in range(PAIRS):
                    mm = pe.matmul(bank_b[:, p * P:(p + 1) * P], K.ones[:, :], diag[:, p, :], start=True, stop=True)
                mm.then_inc(mb_ok, 1)
                entry(c, e1 + 2)
                entry(c, e1 + 3)
                wait_past(pe, ct_done, c)
                for i in range(CHUNK):
                    pe.wait_ge(k_exp, CHUNK * c + i + 1)
                    for p in range(PAIRS):
                        mm = pe.matmul(ct[p // 2][:, p % 2, :], kbuf[:, i, p * P:(p + 1) * P], vbuf[:, i, p, :],
                                       start=(i == 0 and p % 2 == 0), stop=(i == CHUNK - 1), skip_group_check=True)
                    if i < 3:
                        entry(c, e1 + 4 + i)
                mm.then_inc(ct_ok, 1)

            pe.wait_ge(ones_ok, 1)
            chunks(pe, chunk)

        @block.scalar
        def _(act):
            def chunk(c):
                act.copy(rq[:, :], K.rq[:, bass.ds(CHUNK * c, CHUNK)]).then_inc(rq_ok, 1)
                act.copy(pad_bias[:, :], K.pad_bias[:, bass.ds(CHUNK * c, CHUNK)]).then_inc(rq_ok, 1)
                act.wait_ge(rq_ok, 2 * c + 2)
                for i in range(CHUNK):
                    t = CHUNK * c + i
                    act.wait_ge(tp_ok, t + 1)
                    wait_past(act, v_ok, t)
                    act.copy(x_t[:, :, :], tp[:, :, :]).then_inc(xt_ok, 1)
                    act.wait_ge(q_sub, t + 1)
                    act.activation(q_exp[:, :, :], q_exp[:, :, :], ACT.Exp, scale=rq[:, i:i + 1]).then_inc(q_exp_ok, 1)
                    act.wait_ge(k_ok, t + 1)
                    if i == 0:
                        wait_past(act, ct_ok, c)
                    act.activation(kbuf[:, i, :], bank_b[:, :], ACT.Identity, bias=pad_bias[:, i:i + 1],
                                   scale=rq[:, i:i + 1]).then_inc(k_in, 1)
                    act.wait_ge(v_ok, t + 1)
                    act.activation(vbuf[:, i, :, 0:P], bank_a[:, :].rearrange("p (a b) -> p a b", a=PAIRS), ACT.Copy,
                                   scale=rq[:, i:i + 1]).then_inc(v_in, 1)
                act.wait_ge(m_chain, 3 * c + 2)
                act.activation(decay[:, :], m_step[:, :], ACT.Exp).then_inc(decay_ok, 1)
                for i in range(CHUNK):
                    act.wait_ge(k_less, CHUNK * c + i + 1)
                    act.activation(kbuf[:, i, :], kbuf[:, i, :], ACT.Exp).then_inc(k_exp, 1)

            chunks(act, chunk)

        @block.vector
        def _(dve):
            def pick(c, e):
                n, slot = PER_CHUNK * c + e, e % RING
                col = dve.value_load(K.ent[0:1, 0, bass.ds(n, 1)], min_val=0, max_val=EDGE_COLS - GROUP)
                win = dve.value_load(K.ent[0:1, 1, bass.ds(n, 1)], min_val=0, max_val=TILES - 1)
                wait_past(dve, ag_ok, n - RING + 1)
                for u in range(GROUP):
                    ins = dve.tensor_scalar(picks[:, slot, u, :], K.iota16[:, :], K.dst[:, bass.ds(col + u, 1)],
                                            K.base[:, bass.ds(win, 1)], ALU.subtract, ALU.is_equal)
                ins.then_inc(picks_ok, 1)

            def take(c, e):
                n = PER_CHUNK * c + e
                win = dve.value_load(K.ent[0:1, 1, bass.ds(n, 1)], min_val=0, max_val=TILES - 1)
                wait_past(dve, acc_ok, n)
                dve.wait_ge(ag_ok, n + 1)
                deg = K.deg[:, bass.ds(win, 1)]
                dve.tensor_tensor(deg, deg, dg[:, e % 2:e % 2 + 1], ALU.add).then_inc(deg_ok, 1)
                acc = flat(K.acc[:, bass.ds(win, 1), :])
                dve.tensor_tensor(acc, acc, ag[e % 2][:, :], ALU.add).then_inc(acc_ok, 1)
                if e + AHEAD < PER_CHUNK:
                    pick(c, e + AHEAD)
                else:
                    pick(c + 1, e + AHEAD - PER_CHUNK)

            def chunk(c):
                for i in range(CHUNK):
                    t, e0 = CHUNK * c + i, PER_STEP * i
                    for e in range(3):
                        take(c, e0 + e)
                    dve.wait_ge(q_ok, t + 1)
                    q_ps = bank_a[:, :].rearrange("p (a b) -> p a b", a=HEADS)
                    dve.tensor_reduce(q_top[:, :], q_ps, AX.X, ALU.max).then_inc(q_chain, 1)
                    dve.wait_ge(q_chain, 3 * t + 1)
                    dve.tensor_tensor(q_exp[:, :, :], q_ps, bcast(q_top[:, :], HEAD_DIM), ALU.subtract).then_inc(q_sub, 1)
                    take(c, e0 + 3)
                    take(c, e0 + 4)
                    dve.wait_ge(q_exp_ok, t + 1)
                    dve.tensor_reduce(q_sum[:, :], q_exp[:, :, :], AX.X, ALU.add).then_inc(q_chain, 1)
                    dve.wait_ge(q_chain, 3 * t + 2)
                    dve.reciprocal(q_sum[:, :], q_sum[:, :]).then_inc(q_chain, 1)
                    dve.wait_ge(q_chain, 3 * t + 3)
                    wait_past(dve, q_st, 16 * t)
                    dve.tensor_tensor(q[:, :, :], q_exp[:, :, :], bcast(q_sum[:, :], HEAD_DIM), ALU.mult).then_inc(q_done, 1)
                    take(c, e0 + 5)
                    dve.wait_ge(k_in, t + 1)
                    wait_past(dve, kmax_ok, t)
                    dve.tensor_tensor(K.kmax[:, :], K.kmax[:, :], kbuf[:, i, :], ALU.max).then_inc(kmax_ok, 1)
                    take(c, e0 + 6)
                    take(c, e0 + 7)
                e1 = PER_STEP * CHUNK
                dve.wait_ge(kt_ok, c + 1)
                dve.tensor_reduce(m_new[:, :], bank_a[:, :].rearrange("p (a b) -> p a b", a=PAIRS), AX.X,
                                  ALU.max).then_inc(m_chain, 1)
                dve.wait_ge(m_chain, 3 * c + 1)
                dve.tensor_tensor(m_step[:, :], K.m_old[:, :], m_new[:, :], ALU.subtract).then_inc(m_chain, 1)
                dve.wait_ge(m_chain, 3 * c + 2)
                dve.tensor_copy(K.m_old[:, :], m_new[:, :]).then_inc(m_chain, 1)
                dve.wait_ge(q_done, CHUNK * (c + 1))
                for p in range(PAIRS):
                    ins = dve.tensor_scalar(diag[:, p, :], K.ident[:, :], m_new[:, p:p + 1], None, ALU.mult)
                ins.then_inc(diag_ok, 1)
                for e in range(3):
                    take(c, e1 + e)
                dve.wait_ge(mb_ok, c + 1)
                for i in range(CHUNK):
                    dve.tensor_tensor(kbuf[:, i, :], kbuf[:, i, :], bank_b[:, :], ALU.subtract).then_inc(k_less, 1)
                    if i < 4:
                        take(c, e1 + 3 + i)
                dve.wait_ge(decay_ok, c + 1)
                dve.wait_ge(ct_ok, c + 1)
                for p in range(PAIRS):
                    ins = dve.scalar_tensor_tensor(out=K.context[:, p, :], in0=K.context[:, p, :],
                                                   scalar=decay[:, p:p + 1], in1=ct[p // 2][:, p % 2, :],
                                                   op0=ALU.mult, op1=ALU.add)
                ins.then_inc(ct_done, 1)

            for e in range(AHEAD):
                pick(0, e)
            chunks(dve, chunk)


def next_round(nc, K, D):
    with ExitStack() as ctx:
        m = Memory(nc, ctx, "list")
        begun, holds = m.sb("begun", [G_PART, ENTRIES]), m.sb("holds", [G_PART, G_BLOCKS, ENTRIES])
        wrow = m.sb("wrow", [1, ENTRIES])
        psum_e = [m.ps(f"psum_e{i}", [1, 512]) for i in range(3)]
        link_ok, holds_ok, ent_ok = m.sem("link_ok"), m.sem("holds_ok"), m.sem("ent_ok")
        block = ctx.enter_context(nc.Block())

        @block.tensor
        def _(pe):
            pe.wait_ge(holds_ok, 1)
            entry_sums(pe, K, psum_e, holds).then_inc(ent_ok, 1)

        @block.vector
        def _(dve):
            done = [0]

            def link(ins):
                done[0] += 1
                ins.then_inc(link_ok, 1)
                dve.wait_ge(link_ok, done[0])

            link(dve.tensor_scalar(K.gstart[:, :], K.gstart[:, :], -float(ENTRIES), None, ALU.add))
            link(dve.tensor_scalar(K.gend[:, :], K.gend[:, :], -float(ENTRIES), None, ALU.add))
            link(dve.tensor_tensor(K.lhs[:, 1, :], K.gfirst[:, :], K.gstart[:, :], ALU.subtract))
            entry_groups(dve, link, K, begun, holds).then_inc(holds_ok, 1)
            dve.wait_ge(ent_ok, 1)
            entry_values(dve, link, K, psum_e, wrow)

    with ExitStack() as ctx:
        m = Memory(nc, ctx, "further")
        rows, picks = m.sb("rows", [P, GROUP, 2 * DIM], F16), m.sb("picks", [P, GROUP, P], F16)
        cols = m.sb("cols", [P, GROUP], I32)
        ag, dg = m.ps("ag", [P, DIM]), m.ps("dg", [P, 512])
        g_in, col_ok, picks_ok, ag_ok, acc_ok, spare = (m.sem(s) for s in (
            "g_in", "col_ok", "picks_ok", "ag_ok", "acc_ok", "spare"))
        block = ctx.enter_context(nc.Block())

        @block.gpsimd
        def _(pool):
            def entry(n):
                group = pool.value_load(K.ent[0:1, 0, bass.ds(n, 1)], min_val=0, max_val=EDGE_COLS - GROUP)
                wait_past(pool, ag_ok, n)
                pool.tensor_copy(cols[:, :], K.src[:, bass.ds(group, GROUP)]).then_inc(col_ok, 1)
                pool.wait_ge(col_ok, n + 1)
                pool.sem_inc(spare, 1)
                for u in range(GROUP):
                    pool.indirect_dma_start(rows[:, u, :], None, D["table"],
                                            bass.IndirectOffsetOnAxis(ap=cols[:, u:u + 1], axis=0)).then_inc(g_in, 16)

            entry(0)
            with pool.Fori(1, ENTRIES) as n:
                entry(n)

        @block.tensor
        def _(pe):
            def entry(n):
                pe.wait_ge(g_in, 16 * GROUP * (n + 1))
                pe.wait_ge(picks_ok, n + 1)
                wait_past(pe, acc_ok, n)
                for u in range(GROUP):
                    for h in range(2):
                        pe.matmul(ag[:, :], picks[:, u, :], rows[:, u, h * DIM:(h + 1) * DIM],
                                  start=(u == 0 and h == 0), stop=(u == GROUP - 1 and h == 1))
                for u in range(GROUP):
                    mm = pe.matmul(dg[:, 0:1], picks[:, u, :], K.ones16[:, :], start=(u == 0), stop=(u == GROUP - 1))
                mm.then_inc(ag_ok, 1)

            entry(0)
            with pe.Fori(1, ENTRIES) as n:
                entry(n)

        @block.vector
        def _(dve):
            def entry(n):
                col = dve.value_load(K.ent[0:1, 0, bass.ds(n, 1)], min_val=0, max_val=EDGE_COLS - GROUP)
                win = dve.value_load(K.ent[0:1, 1, bass.ds(n, 1)], min_val=0, max_val=TILES - 1)
                wait_past(dve, acc_ok, n)
                for u in range(GROUP):
                    ins = dve.tensor_scalar(picks[:, u, :], K.iota16[:, :], K.dst[:, bass.ds(col + u, 1)],
                                            K.base[:, bass.ds(win, 1)], ALU.subtract, ALU.is_equal)
                ins.then_inc(picks_ok, 1)
                dve.wait_ge(ag_ok, n + 1)
                acc = flat(K.acc[:, bass.ds(win, 1), :])
                dve.tensor_tensor(acc, acc, ag[:, :], ALU.add)
                deg = K.deg[:, bass.ds(win, 1)]
                dve.tensor_tensor(deg, deg, dg[:, 0:1], ALU.add).then_inc(acc_ok, 1)

            entry(0)
            with dve.Fori(1, ENTRIES) as n:
                entry(n)


def fold(nc, K, D):
    with ExitStack() as ctx:
        m = Memory(nc, ctx, "fold")
        w32 = m.sb("w32", [P, 2, KC, DIM])
        wo = m.sb("wo", [P, KC, DIM])
        wmax, wall, wscale = m.sb("wmax", [P, 1]), m.sb("wall", [P, 1]), m.sb("wscale", [P, 1])
        wbits = m.sb("wbits", [P, 1], I32)
        k_inv = m.sb("k_inv", [P, PAIRS])
        heads = m.sb("heads", [P, PAIRS, P])
        heads_t = m.sb("heads_t", [P, PAIRS, P])
        tp = m.ps("tp", [P, PAIRS, P])
        c2 = [m.ps(f"c2_{i}", [P, DIM]) for i in range(PAIRS)]
        w_in, o_in, v_in = m.sem("w_in"), m.sem("o_in"), m.sem("v_in")
        link_ok, wmax_ok, wall_ok = m.sem("link_ok"), m.sem("wmax_ok"), m.sem("wall_ok")
        heads_ok, tp_ok, heads_t_ok, c2_ok, c2_in = (m.sem(s) for s in ("heads_ok", "tp_ok", "heads_t_ok", "c2_ok", "c2_in"))
        block = ctx.enter_context(nc.Block())

        @block.sync
        def _(sp):
            sp.dma_start(w32[:, 0, :, :], D["w_self"]).then_inc(w_in, 16)
            sp.dma_start(w32[:, 1, :, :], D["w_neigh"]).then_inc(w_in, 16)
            sp.dma_start(wo[:, :, :], D["w_out"]).then_inc(o_in, 16)
            for i, name in enumerate(("bias", "gamma", "beta", "out_gamma")):
                sp.dma_start(K.vec[:, i, :], D[name].to_broadcast([P, DIM])).then_inc(v_in, 16)
            sp.dma_start(K.wg[:, :, :], D["w_gate"]).then_inc(v_in, 16)
            sp.dma_start(K.bg[:, :], D["b_gate"].to_broadcast([P, EXPERTS])).then_inc(v_in, 16)
            sp.wait_ge(v_in, 96)

        @block.gpsimd
        def _(pool):
            pool.wait_ge(wmax_ok, 1)
            pool.partition_all_reduce(wall[:, :], wmax[:, :], P, MAX_ALL).then_inc(wall_ok, 1)

        @block.tensor
        def _(pe):
            pe.wait_ge(heads_ok, 1)
            for p in range(PAIRS):
                mm = pe.transpose(tp[:, p, :], heads[:, p, :], K.ident[:, :])
            mm.then_inc(tp_ok, 1)
            pe.wait_ge(heads_t_ok, 1)
            pe.wait_ge(o_in, 16)
            for p in range(PAIRS):
                mm = pe.matmul(c2[p][:, :], heads_t[:, p, :], wo[:, p, :], start=True, stop=True)
            mm.then_inc(c2_ok, 1)

        @block.scalar
        def _(act):
            act.wait_ge(tp_ok, 1)
            act.copy(heads_t[:, :, :], tp[:, :, :]).then_inc(heads_t_ok, 1)
            act.wait_ge(c2_ok, 1)
            for p in range(PAIRS):
                act.copy(K.c2[:, p, :], c2[p][:, :]).then_inc(c2_in, 1)

        @block.vector
        def _(dve):
            done = [0]

            def link(ins):
                done[0] += 1
                ins.then_inc(link_ok, 1)
                dve.wait_ge(link_ok, done[0])

            link(dve.memset(flat(heads[:, :, :]), 0.0))
            link(dve.reciprocal(k_inv[:, :], K.context[:, :, P]))
            link(dve.tensor_scalar(k_inv[:, :], k_inv[:, :], HEAD_DIM ** -0.5, None, ALU.mult))
            for p in range(PAIRS):
                for h in range(2):
                    r = slice(h * HEAD_DIM, (h + 1) * HEAD_DIM)
                    link(dve.tensor_scalar(heads[r, p, r], K.context[r, p, r], k_inv[r, p:p + 1], None, ALU.mult))
            dve.sem_inc(heads_ok, 1)
            link(dve.tensor_scalar(K.deg[:, :], K.deg[:, :], 1.0, None, ALU.max))
            link(dve.reciprocal(K.deg[:, :], K.deg[:, :]))
            link(dve.tensor_scalar(K.run[:, :], K.pos[:, 0:EXPERTS], float(BUCKET), None, ALU.mult))
            link(dve.tensor_scalar(K.falling[:, :], K.pos[:, 0:EXPERTS], -1.0, float(EXPERTS), ALU.mult, ALU.add))
            dve.wait_ge(w_in, 32)
            dve.tensor_reduce(wmax[:, :], w32[:, :, :, :].rearrange("p a b c -> p (a b c)"), AX.X, ALU.max,
                              apply_absolute_value=True).then_inc(wmax_ok, 1)
            dve.wait_ge(wall_ok, 1)
            power_of_two(dve, link, wscale[:, :], wall[:, :], K.unscale[:, :], wbits[:, :])
            link(dve.tensor_scalar(K.unscale[:, :], K.unscale[:, :], 1.0 / XS, None, ALU.mult))
            w = w32[:, :, :, :].rearrange("p a b c -> p (a b c)")
            hi, lo = (x[:, :, :, :].rearrange("p a b c -> p (a b c)") for x in (K.wn_hi, K.wn_lo))
            link(dve.tensor_scalar(hi, w, wscale[:, :], None, ALU.mult))
            link(dve.scalar_tensor_tensor(out=lo, in0=w, scalar=wscale[:, :], in1=hi, op0=ALU.mult, op1=ALU.subtract))


def mix(nc, K, D):
    with ExitStack() as ctx:
        m = Memory(nc, ctx, "mix")
        xrow, x_t = m.sb("xrow", [P, 2 * KC, P], F16), m.sb("x_t", [P, 2, 2 * KC, P], F16)
        qrow, q_t = m.sb("qrow", [P, KC, P]), m.sb("q_t", [P, 2, KC, P])
        mean, halves = m.sb("mean", [P, DIM]), m.sb("halves", [P, 2 * KC, P], F16)
        m_t = m.sb("m_t", [P, 2, 2 * KC, P], F16)
        xres = m.sb("xres", [P, DIM])
        h, hn, hg, on = (m.sb(s, [P, DIM]) for s in ("h", "hn", "hg", "on"))
        stats, mv = m.sb("stats", [P, 2, 6]), m.sb("mv", [P, 2, 2])
        rstd, sd, shift = m.sb("rstd", [P, 2]), m.sb("sd", [P, 2]), m.sb("shift", [P, 2])
        stats1, mv1, sd1 = m.sb("stats1", [P, 6]), m.sb("mv1", [P, 2]), m.sb("sd1", [P, 1])
        x1 = m.sb("x1", [P, CHUNK, X1W])
        y, y_t = m.sb("y", [P, CHUNK, KC, P]), m.sb("y_t", [P, KC, P])
        logit, top, hot = m.sb("logit", [P, EXPERTS]), m.sb("top", [P, 1]), m.sb("hot", [P, EXPERTS])
        place, slot_f = m.sb("place", [P, EXPERTS]), m.sb("slot_f", [P, 1])
        slots, ids = m.sb("slots", [P, 1], I32), m.sb("ids", [P, 1], I32)
        tpx, tpm = m.ps("tpx", [P, 2 * KC, P], F16), m.ps("tpm", [P, 2 * KC, P], F16)
        tpq, tpy = m.ps("tpq", [P, KC, P]), m.ps("tpy", [P, KC, P])
        g, o = m.ps("g", [P, DIM]), m.ps("o", [P, DIM])
        small = m.ps("small", [P, 512])
        lg, rank, total = small[:, 0:8], small[:, 8:16], small[:, 16:24]
        S = Names()
        S.ids_st = K.ids_st
        (S.xr_in, S.q_in, S.xres_in, S.tpx_ok, S.tpq_ok, S.tpm_ok, S.x_t_ok, S.q_t_ok, S.m_t_ok, S.mean_ok,
         S.hi_ok, S.lo_ok, S.g_ok, S.o_ok, S.h_ok, S.var_ok, S.sd_ok, S.norm_ok, S.hn_ok, S.on_ok, S.sum_ok,
         S.x1_ok, S.var1_ok, S.sd1_ok, S.norm1_ok, S.y_ok, S.tpy_ok, S.y_t_ok, S.lg_ok, S.hot_ok, S.rank_ok,
         S.slot_ok, S.chain_a, S.chain_b, S.chain_c, S.chain_d, S.x1_st, S.spare, S.ids_ok) = (
            m.sem(name) for name in (
             "xr_in q_in xres_in tpx_ok tpq_ok tpm_ok x_t_ok q_t_ok m_t_ok mean_ok hi_ok lo_ok g_ok o_ok h_ok "
             "var_ok sd_ok norm_ok hn_ok on_ok sum_ok x1_ok var1_ok sd1_ok norm1_ok y_ok tpy_ok y_t_ok lg_ok "
             "hot_ok rank_ok slot_ok chain_a chain_b chain_c chain_d x1_st spare ids_ok").split())
        LAG_GO, LAG_TAIL = 1, 3
        block = ctx.enter_context(nc.Block())

        @block.sync
        def _(sp):
            def load(t):
                wait_past(sp, S.tpx_ok, t)
                sp.dma_start(flat(xrow[:, :, :]), D["table"][bass.ds(t * P, P), :]).then_inc(S.xr_in, 16)
                wait_past(sp, S.tpq_ok, t)
                sp.dma_start(flat(qrow[:, :, :]), D["q"][bass.ds(t * P, P), :]).then_inc(S.q_in, 16)

            def body(t, i):
                if (a := stage(TILES, t, 0)) is not None:
                    load(a)
                if (a := stage(TILES, t, LAG_GO)) is not None:
                    wait_past(sp, S.sum_ok, a)
                    sp.dma_start(xres[:, :], D["x"][bass.ds(a * P, P), :]).then_inc(S.xres_in, 16)
                if (a := stage(TILES, t, LAG_TAIL)) is not None:
                    sp.wait_ge(S.hot_ok, a + 1)
                    sp.dma_start(D["x1"][bass.ds(a * P, P), :], x1[:, (i - LAG_TAIL) % CHUNK, :]).then_inc(S.x1_st, 16)

            in_turn(sp, TILES, CHUNK, LAG_TAIL, body)
            sp.wait_ge(S.x1_st, 16 * TILES)

        @block.gpsimd
        def _(pool):
            def body(t, i):
                if (a := stage(TILES, t, LAG_GO)) is not None:
                    pool.wait_ge(S.xres_in, 16 * (a + 1))
                    pool.tensor_tensor(xres[:, :], xres[:, :], K.vec[:, 2, :], ALU.add).then_inc(S.chain_c, 1)
                    pool.wait_ge(S.hn_ok, a + 1)
                    wait_past(pool, S.x1_ok, a)
                    pool.tensor_tensor(hg[:, :], hn[:, :], K.vec[:, 1, :], ALU.mult).then_inc(S.chain_c, 1)
                    pool.wait_ge(S.chain_c, 2 * a + 2)
                    pool.tensor_tensor(hg[:, :], hg[:, :], xres[:, :], ALU.add).then_inc(S.sum_ok, 1)
                if (a := stage(TILES, t, LAG_TAIL)) is not None:
                    pool.wait_ge(S.slot_ok, a + 1)
                    pool.sem_inc(S.spare, 1)
                    pool.indirect_dma_start(D["perm"], bass.IndirectOffsetOnAxis(ap=slots[:, :], axis=0),
                                            ids[:, :], None).then_inc(S.ids_st, 16)

            in_turn(pool, TILES, CHUNK, LAG_TAIL, body)
            pool.wait_ge(S.ids_st, 16 * TILES)

        @block.tensor
        def _(pe):
            def body(t, i):
                tile, go, tail = (stage(TILES, t, n) for n in (0, LAG_GO, LAG_TAIL))
                if tail is not None:
                    pe.wait_ge(S.y_ok, tail + 1)
                    wait_past(pe, S.y_t_ok, tail)
                    for k in range(KC):
                        mm = pe.transpose(tpy[:, k, :], y[:, (i - LAG_TAIL) % CHUNK, k, :], K.ident[:, :])
                    mm.then_inc(S.tpy_ok, 1)
                if tile is not None:
                    pe.wait_ge(S.xr_in, 16 * (tile + 1))
                    wait_past(pe, S.x_t_ok, tile)
                    for k in range(2 * KC):
                        mm = pe.transpose(tpx[:, k, :], xrow[:, k, :], K.ident16[:, :])
                    mm.then_inc(S.tpx_ok, 1)
                    pe.wait_ge(S.q_in, 16 * (tile + 1))
                    wait_past(pe, S.q_t_ok, tile)
                    for k in range(KC):
                        mm = pe.transpose(tpq[:, k, :], qrow[:, k, :], K.ident[:, :])
                    mm.then_inc(S.tpq_ok, 1)
                if tail is not None:
                    pe.wait_ge(S.y_t_ok, tail + 1)
                    wait_past(pe, S.slot_ok, tail)
                    for k in range(KC):
                        mm = pe.matmul(lg, y_t[:, k, :], K.wg[:, k, :], start=(k == 0), stop=(k == KC - 1))
                    mm.then_inc(S.lg_ok, 1)
                if go is not None:
                    b = (i - LAG_GO) % CHUNK % 2
                    pe.wait_ge(S.x_t_ok, go + 1)
                    pe.wait_ge(S.m_t_ok, go + 1)
                    wait_past(pe, S.h_ok, go)
                    todo = [(src, w, a, half, k) for src, w in ((x_t, 0), (m_t, 1)) for k in range(KC)
                            for a, half in ((0, K.wn_hi), (0, K.wn_lo), (KC, K.wn_hi))]
                    for j, (src, w, a, half, k) in enumerate(todo):
                        mm = pe.matmul(g[:, :], src[:, b, a + k, :], half[:, w, k, :], start=(j == 0),
                                       stop=(j == len(todo) - 1))
                    mm.then_inc(S.g_ok, 1)
                    pe.wait_ge(S.q_t_ok, go + 1)
                    wait_past(pe, S.on_ok, go)
                    for k in range(KC):
                        mm = pe.matmul(o[:, :], q_t[:, b, k, :], K.c2[:, k, :], start=(k == 0), stop=(k == KC - 1))
                    mm.then_inc(S.o_ok, 1)
                if tile is not None:
                    pe.wait_ge(S.lo_ok, tile + 1)
                    wait_past(pe, S.m_t_ok, tile)
                    for k in range(2 * KC):
                        mm = pe.transpose(tpm[:, k, :], halves[:, k, :], K.ident16[:, :])
                    mm.then_inc(S.tpm_ok, 1)
                if tail is not None:
                    pe.wait_ge(S.hot_ok, tail + 1)
                    pe.matmul(rank, K.upper[:, :], hot[:, :], start=True, stop=True)
                    pe.matmul(total, K.ones[:, :], hot[:, :], start=True, stop=True).then_inc(S.rank_ok, 1)

            in_turn(pe, TILES, CHUNK, LAG_TAIL, body)

        @block.scalar
        def _(act):
            def body(t, i):
                tile, go, tail = (stage(TILES, t, n) for n in (0, LAG_GO, LAG_TAIL))
                if tail is not None:
                    act.wait_ge(S.tpy_ok, tail + 1)
                    wait_past(act, S.lg_ok, tail)
                    act.copy(y_t[:, :, :], tpy[:, :, :]).then_inc(S.y_t_ok, 1)
                if tile is not None:
                    act.wait_ge(S.mean_ok, tile + 1)
                    wait_past(act, S.tpm_ok, tile)
                    act.copy(flat(halves[:, 0:KC, :]), mean[:, :]).then_inc(S.hi_ok, 1)
                    act.wait_ge(S.tpx_ok, tile + 1)
                    wait_past(act, S.g_ok, count_before(tile, i))
                    act.copy(x_t[:, i % 2, :, :], tpx[:, :, :]).then_inc(S.x_t_ok, 1)
                    act.wait_ge(S.tpq_ok, tile + 1)
                    wait_past(act, S.o_ok, count_before(tile, i))
                    act.copy(q_t[:, i % 2, :, :], tpq[:, :, :]).then_inc(S.q_t_ok, 1)
                if go is not None:
                    n = (i - LAG_GO) % CHUNK
                    act.wait_ge(S.var_ok, go + 1)
                    act.activation(sd[:, :], rstd[:, :], ACT.Sqrt).then_inc(S.sd_ok, 1)
                    act.wait_ge(S.norm_ok, go + 1)
                    wait_past(act, S.sum_ok, go)
                    act.activation(hn[:, :], h[:, :], ACT.Identity, bias=shift[:, 0:1], scale=rstd[:, 0:1]).then_inc(S.hn_ok, 1)
                    act.activation(on[:, :], o[:, :], ACT.Identity, bias=shift[:, 1:2], scale=rstd[:, 1:2]).then_inc(S.on_ok, 1)
                    act.wait_ge(S.var1_ok, go + 1)
                    act.activation(sd1[:, :], x1[:, n, DIM:DIM + 1], ACT.Sqrt).then_inc(S.sd1_ok, 1)
                    act.wait_ge(S.norm1_ok, go + 1)
                    act.activation(y[:, n, :, :].rearrange("p a b -> p (a b)"), x1[:, n, 0:DIM], ACT.Identity,
                                   bias=x1[:, n, DIM + 1:DIM + 2], scale=x1[:, n, DIM:DIM + 1]).then_inc(S.y_ok, 1)

            in_turn(act, TILES, CHUNK, LAG_TAIL, body)

        @block.vector
        def _(dve):
            dve.memset(x1[:, :, DIM:X1W], 0.0).then_inc(S.ids_ok, 1)
            dve.tensor_copy(ids[:, :], K.node[:, :]).then_inc(S.ids_ok, 1)
            dve.wait_ge(S.ids_ok, 2)

            def body(t, i):
                tile, go, tail = (stage(TILES, t, n) for n in (0, LAG_GO, LAG_TAIL))
                if tile is not None:
                    wait_past(dve, S.lo_ok, tile)
                    wait_past(dve, S.hi_ok, tile)
                    dve.tensor_scalar(mean[:, :], flat(K.acc[:, bass.ds(tile, 1), :]), K.deg[:, bass.ds(tile, 1)], None,
                                      ALU.mult).then_inc(S.mean_ok, 1)
                    dve.wait_ge(S.hi_ok, tile + 1)
                    dve.tensor_tensor(flat(halves[:, KC:, :]), mean[:, :], flat(halves[:, 0:KC, :]),
                                      ALU.subtract).then_inc(S.lo_ok, 1)
                if tail is not None:
                    link = Chain(dve, S.chain_b, 4, tail)
                    rest = x1[:, (i - LAG_TAIL) % CHUNK, DIM + 2:DIM + 2 + EXPERTS]
                    dve.wait_ge(S.lg_ok, tail + 1)
                    link(dve.tensor_tensor(logit[:, :], lg, K.bg[:, :], ALU.add))
                    link(dve.tensor_reduce(top[:, :], logit[:, :], AX.X, ALU.max))
                    dve.tensor_scalar(rest, logit[:, :], top[:, :], None, ALU.subtract)
                    link(dve.scalar_tensor_tensor(out=logit[:, :], in0=logit[:, :], scalar=top[:, :],
                                                  in1=K.falling[:, :], op0=ALU.is_equal, op1=ALU.mult))
                    link(dve.tensor_reduce(top[:, :], logit[:, :], AX.X, ALU.max))
                    dve.tensor_scalar(hot[:, :], logit[:, :], top[:, :], None, ALU.is_equal).then_inc(S.hot_ok, 1)
                if tile is not None:
                    dve.wait_ge(S.tpm_ok, tile + 1)
                    wait_past(dve, S.g_ok, count_before(tile, i))
                    dve.tensor_copy(m_t[:, i % 2, :, :], tpm[:, :, :]).then_inc(S.m_t_ok, 1)
                if go is not None:
                    n = (i - LAG_GO) % CHUNK
                    link = Chain(dve, S.chain_a, 8, go)
                    dve.wait_ge(S.g_ok, go + 1)
                    dve.scalar_tensor_tensor(out=h[:, :], in0=g[:, :], scalar=K.unscale[:, :], in1=K.vec[:, 0, :],
                                             op0=ALU.mult, op1=ALU.add).then_inc(S.h_ok, 1)
                    dve.wait_ge(S.h_ok, go + 1)
                    dve.bn_stats(stats[:, 0, :], h[:, :])
                    dve.wait_ge(S.o_ok, go + 1)
                    link(dve.bn_stats(stats[:, 1, :], o[:, :]))
                    dve.sem_inc(S.spare, 1)
                    dve.bn_aggr(mv[:, 0, :], stats[:, 0, :])
                    link(dve.bn_aggr(mv[:, 1, :], stats[:, 1, :]))
                    dve.tensor_scalar(rstd[:, :], mv[:, :, 1], EPS, None, ALU.add).then_inc(S.var_ok, 1)
                    dve.wait_ge(S.sd_ok, go + 1)
                    link(dve.reciprocal(rstd[:, :], sd[:, :]))
                    link(dve.tensor_tensor(shift[:, :], mv[:, :, 0], rstd[:, :], ALU.mult))
                    dve.tensor_scalar(shift[:, :], shift[:, :], -1.0, None, ALU.mult).then_inc(S.norm_ok, 1)
                    wait_past(dve, S.x1_st, 16 * (go - CHUNK + 1))
                    dve.wait_ge(S.on_ok, go + 1)
                    link(dve.tensor_tensor(on[:, :], on[:, :], K.vec[:, 3, :], ALU.mult))
                    dve.wait_ge(S.sum_ok, go + 1)
                    dve.tensor_tensor(x1[:, n, 0:DIM], on[:, :], hg[:, :], ALU.add).then_inc(S.x1_ok, 1)
                    dve.wait_ge(S.x1_ok, go + 1)
                    link(dve.bn_stats(stats1[:, :], x1[:, n, 0:DIM]))
                    dve.sem_inc(S.spare, 1)
                    link(dve.bn_aggr(mv1[:, :], stats1[:, :]))
                    dve.tensor_scalar(x1[:, n, DIM:DIM + 1], mv1[:, 1:2], EPS, None, ALU.add).then_inc(S.var1_ok, 1)
                    dve.wait_ge(S.sd1_ok, go + 1)
                    link(dve.reciprocal(x1[:, n, DIM:DIM + 1], sd1[:, :]))
                    dve.scalar_tensor_tensor(out=x1[:, n, DIM + 1:DIM + 2], in0=mv1[:, 0:1], scalar=-1.0,
                                             in1=x1[:, n, DIM:DIM + 1], op0=ALU.mult, op1=ALU.mult).then_inc(S.norm1_ok, 1)
                if tail is not None:
                    link = Chain(dve, S.chain_d, 4, tail)
                    dve.wait_ge(S.rank_ok, tail + 1)
                    wait_past(dve, S.ids_st, 16 * tail)
                    link(dve.tensor_tensor(place[:, :], K.run[:, :], rank, ALU.add))
                    link(dve.tensor_tensor(place[:, :], place[:, :], hot[:, :], ALU.mult))
                    link(dve.tensor_reduce(slot_f[:, :], place[:, :], AX.X, ALU.add))
                    dve.tensor_copy(slots[:, :], slot_f[:, :])
                    dve.tensor_scalar(ids[:, :], K.node[:, :], 0.0, None, ALU.add)
                    link(dve.tensor_scalar(K.node[:, :], K.node[:, :], float(P), None, ALU.add))
                    dve.tensor_tensor(K.run[:, :], K.run[:, :], total, ALU.add).then_inc(S.slot_ok, 1)
                    dve.wait_ge(S.slot_ok, tail + 1)

            in_turn(dve, TILES, CHUNK, LAG_TAIL, body)


def experts(nc, K, D):
    U = UNROLL
    LAG_Y, LAG_TY, LAG_H, LAG_TH, LAG_F = range(5)
    with ExitStack() as ctx:
        m = Memory(nc, ctx, "experts")
        w1, w2 = m.sb("w1", [P, EXPERTS, KC, HIDDEN]), m.sb("w2", [P, EXPERTS, 2, DIM])
        b1, b2 = m.sb("b1", [P, 2, EXPERTS]), m.sb("b2", [P, EXPERTS, DIM])
        e_row, e_int = m.sb("e_row", [1, 6, EXPERTS]), m.sb("e_int", [1, EXPERTS], I32)
        t_in, t_val = m.sb("t_in", [1, XT, EXPERTS]), m.sb("t_val", [1, 2, XT, EXPERTS])
        t_sum = m.sb("t_sum", [1, 3, XT])
        lots = m.sb("lots", [1, 2, XT], I32)
        idx = m.sb("idx", [P, U], I32)
        rows, out = m.sb("rows", [P, U, X1W]), m.sb("out", [P, U, DIM])
        y, y_t = m.sb("y", [P, 2, KC, P]), m.sb("y_t", [P, 2, KC, P])
        h, h_t, f = m.sb("h", [P, 2, HIDDEN]), m.sb("h_t", [P, 2, 2, P]), m.sb("f", [P, DIM])
        ex, score = m.sb("ex", [P, EXPERTS]), m.sb("score", [P, U])
        tpy = [m.ps(f"tpy{i}", [P, KC, P]) for i in range(2)]
        hp = [m.ps(f"hp{i}", [P, HIDDEN]) for i in range(2)]
        tph = [m.ps(f"tph{i}", [P, 2, P]) for i in range(2)]
        fp = [m.ps(f"fp{i}", [P, DIM]) for i in range(2)]
        S = Names()
        (S.w_in, S.b_in, S.link_ok, S.lots_ok, S.cleared, S.y_ok, S.sum_ok, S.score_ok, S.tpy_ok, S.y_t_ok,
         S.hp_ok, S.h_ok, S.tph_ok, S.h_t_ok, S.fp_ok, S.f_ok, S.out_ok, S.spare, S.gone) = (
            m.sem(name) for name in (
             "w_in b_in link_ok lots_ok cleared y_ok sum_ok score_ok tpy_ok y_t_ok hp_ok h_ok tph_ok h_t_ok "
             "fp_ok f_ok out_ok spare gone").split())
        idx_in, rows_in, out_st = m.sems("idx_in", U), K.rows_in, K.out_st
        block = ctx.enter_context(nc.Block())

        def turns(t, i):
            return t // U + 1 if isinstance(t, int) else (t - i) // U + 1

        @block.sync
        def _(sp):
            sp.dma_start(w1[:, :, :, :], D["w1"]).then_inc(S.w_in, 16)
            sp.dma_start(w2[:, :, :, :], D["w2"]).then_inc(S.w_in, 16)
            sp.dma_start(b1[:, :, :], D["b1"]).then_inc(S.b_in, 16)
            sp.dma_start(flat(b2[:, :, :]), D["b2"].to_broadcast([P, EXPERTS * DIM])).then_inc(S.b_in, 16)
            sp.wait_ge(S.lots_ok, 1)

            def round_(c):
                for i in range(U):
                    t = U * c + i
                    at = sp.value_load(lots[0:1, 1, bass.ds(t, 1)], min_val=0, max_val=EXPERTS * BUCKET)
                    wait_past(sp, out_st[i], 16 * c)
                    sp.sem_inc(S.gone, 1)
                    sp.dma_start(idx[:, i:i + 1], D["perm"][bass.ds(at, P), :]).then_inc(idx_in[i], 16)

            round_(0)
            with sp.Fori(1, XT // U) as c:
                round_(c)

        @block.gpsimd
        def _(pool):
            pool.memset(rows[:, :, :], 0.0).then_inc(S.cleared, 1)
            pool.wait_ge(S.cleared, 1)

            def round_(c):
                for i in range(U):
                    pool.wait_ge(idx_in[i], 16 * (c + 1))
                    pool.sem_inc(S.spare, 1)
                    pool.indirect_dma_start(rows[:, i, :], None, D["x1"],
                                            bass.IndirectOffsetOnAxis(ap=idx[:, i:i + 1], axis=0),
                                            bounds_check=ROWS - 1, oob_is_err=False).then_inc(rows_in[i], 16)
                    j = (i - 5) % U
                    if i < 5 and isinstance(c, int) and c == 0:
                        continue
                    scatter(U * c + i - 5, j)

            def scatter(t, j):
                pool.wait_ge(S.out_ok, t + 1)
                pool.sem_inc(S.spare, 1)
                pool.indirect_dma_start(D["out"], bass.IndirectOffsetOnAxis(ap=idx[:, j:j + 1], axis=0), out[:, j, :],
                                        None, bounds_check=ROWS - 1, oob_is_err=False).then_inc(out_st[j], 16)

            round_(0)
            with pool.Fori(1, XT // U) as c:
                round_(c)
            for t in range(XT - 5, XT):
                scatter(t, t % U)
            for i in range(U):
                pool.wait_ge(out_st[i], 16 * (XT // U))

        @block.tensor
        def _(pe):
            def body(t, i):
                if (a := stage(XT, t, LAG_TY)) is not None:
                    b = (i - LAG_TY) % 2
                    pe.wait_ge(S.y_ok, a + 1)
                    wait_past(pe, S.y_t_ok, a - 1)
                    for k in range(KC):
                        mm = pe.transpose(tpy[b][:, k, :], y[:, b, k, :], K.ident[:, :])
                    mm.then_inc(S.tpy_ok, 1)
                if (a := stage(XT, t, LAG_H)) is not None:
                    b = (i - LAG_H) % 2
                    e = pe.value_load(lots[0:1, 0, bass.ds(a, 1)], min_val=0, max_val=EXPERTS - 1)
                    pe.wait_ge(S.y_t_ok, a + 1)
                    wait_past(pe, S.h_ok, a - 1)
                    for k in range(KC):
                        mm = pe.matmul(hp[b][:, :], y_t[:, b, k, :], flat(w1[:, bass.ds(e, 1), k, :]), start=(k == 0),
                                       stop=(k == KC - 1))
                    mm.then_inc(S.hp_ok, 1)
                if (a := stage(XT, t, LAG_TH)) is not None:
                    b = (i - LAG_TH) % 2
                    pe.wait_ge(S.h_ok, a + 1)
                    wait_past(pe, S.h_t_ok, a - 1)
                    for k in range(2):
                        mm = pe.transpose(tph[b][:, k, :], h[:, b, k * P:(k + 1) * P], K.ident[:, :])
                    mm.then_inc(S.tph_ok, 1)
                if (a := stage(XT, t, LAG_F)) is not None:
                    b = (i - LAG_F) % 2
                    e = pe.value_load(lots[0:1, 0, bass.ds(a, 1)], min_val=0, max_val=EXPERTS - 1)
                    pe.wait_ge(S.h_t_ok, a + 1)
                    wait_past(pe, S.f_ok, a - 1)
                    for k in range(2):
                        mm = pe.matmul(fp[b][:, :], h_t[:, b, k, :], flat(w2[:, bass.ds(e, 1), k, :]), start=(k == 0),
                                       stop=(k == 1))
                    mm.then_inc(S.fp_ok, 1)

            pe.wait_ge(S.w_in, 32)
            pe.wait_ge(S.lots_ok, 1)
            in_turn(pe, XT, U, LAG_F, body)

        @block.scalar
        def _(act):
            def body(t, i):
                if (a := stage(XT, t, LAG_TY)) is not None:
                    b = (i - LAG_TY) % 2
                    act.wait_ge(S.tpy_ok, a + 1)
                    wait_past(act, S.hp_ok, a - 1)
                    act.copy(y_t[:, b, :, :], tpy[b][:, :, :]).then_inc(S.y_t_ok, 1)
                if (a := stage(XT, t, LAG_H)) is not None:
                    b = (i - LAG_H) % 2
                    act.wait_ge(S.hp_ok, a + 1)
                    wait_past(act, S.tph_ok, a - 1)
                    act.copy(h[:, b, :], hp[b][:, :]).then_inc(S.h_ok, 1)
                if (a := stage(XT, t, LAG_Y)) is not None:
                    act.wait_ge(rows_in[i], 16 * turns(a, i))
                    wait_past(act, S.tpy_ok, a - 1)
                    act.activation(y[:, i % 2, :, :].rearrange("p a b -> p (a b)"), rows[:, i, 0:DIM], ACT.Identity,
                                   bias=rows[:, i, DIM + 1:DIM + 2], scale=rows[:, i, DIM:DIM + 1]).then_inc(S.y_ok, 1)
                    wait_past(act, S.score_ok, a)
                    act.activation(ex[:, :], rows[:, i, DIM + 2:DIM + 2 + EXPERTS], ACT.Exp,
                                   accum_out=score[:, i:i + 1]).then_inc(S.sum_ok, 1)

            in_turn(act, XT, U, LAG_F, body)

        @block.vector
        def _(dve):
            done = [0]

            def link(ins):
                done[0] += 1
                ins.then_inc(S.link_ok, 1)
                dve.wait_ge(S.link_ok, done[0])

            count, tiles, first, after, value, e_num = (e_row[:, k, :] for k in range(6))
            link(dve.tensor_copy(e_num, K.pos[0:1, 0:EXPERTS]))
            link(dve.tensor_scalar(value, e_num, float(-BUCKET), None, ALU.mult))
            link(dve.tensor_tensor(count, K.run[0:1, :], value, ALU.add))
            link(dve.tensor_scalar(e_int[:, :], count, float(P - 1), None, ALU.add))
            link(dve.tensor_scalar(e_int[:, :], e_int[:, :], 7, None, ALU.arith_shift_right))
            link(dve.tensor_copy(tiles, e_int[:, :]))
            link(dve.memset(first, 0.0))
            for e in range(1, EXPERTS):
                link(dve.tensor_tensor(first[:, e:e + 1], first[:, e - 1:e], tiles[:, e - 1:e], ALU.add))
            link(dve.tensor_tensor(after, first, tiles, ALU.add))
            num = bcast(K.pos[0:1, 0:XT], EXPERTS)

            def all_tiles(v):
                return v.unsqueeze(1).to_broadcast([1, XT, EXPERTS])

            link(dve.tensor_tensor(t_in[:, :, :], num, all_tiles(first), ALU.is_ge))
            link(dve.tensor_tensor(t_val[:, 0, :, :], num, all_tiles(after), ALU.is_lt))
            link(dve.tensor_tensor(t_in[:, :, :], t_in[:, :, :], t_val[:, 0, :, :], ALU.mult))
            link(dve.tensor_scalar(count, first, float(-P), float(-EXPERTS * BUCKET), ALU.mult, ALU.add))
            link(dve.tensor_tensor(count, count, value, ALU.subtract))
            link(dve.tensor_tensor(t_val[:, 0, :, :], t_in[:, :, :], all_tiles(e_num), ALU.mult))
            link(dve.tensor_tensor(t_val[:, 1, :, :], t_in[:, :, :], all_tiles(count), ALU.mult))
            link(dve.tensor_reduce(t_sum[:, 0, :], t_in[:, :, :], AX.X, ALU.add))
            link(dve.tensor_reduce(t_sum[:, 1, :], t_val[:, 1, :, :], AX.X, ALU.add))
            link(dve.tensor_reduce(t_sum[:, 2, :], t_val[:, 0, :, :], AX.X, ALU.add))
            link(dve.tensor_tensor(t_sum[:, 0, :], t_sum[:, 0, :], K.pos[0:1, 0:XT], ALU.mult))
            link(dve.tensor_scalar(t_sum[:, 0, :], t_sum[:, 0, :], float(P), float(EXPERTS * BUCKET), ALU.mult, ALU.add))
            link(dve.tensor_tensor(lots[:, 1, :], t_sum[:, 0, :], t_sum[:, 1, :], ALU.add))
            dve.tensor_copy(lots[:, 0, :], t_sum[:, 2, :]).then_inc(S.lots_ok, 1)
            dve.wait_ge(S.lots_ok, 1)
            dve.wait_ge(S.b_in, 32)

            def body(t, i):
                if (a := stage(XT, t, LAG_Y)) is not None:
                    dve.wait_ge(S.sum_ok, a + 1)
                    dve.reciprocal(score[:, i:i + 1], score[:, i:i + 1]).then_inc(S.score_ok, 1)
                if (a := stage(XT, t, LAG_TH)) is not None:
                    b = (i - LAG_TH) % 2
                    e = dve.value_load(lots[0:1, 0, bass.ds(a, 1)], min_val=0, max_val=EXPERTS - 1)
                    dve.wait_ge(S.tph_ok, a + 1)
                    wait_past(dve, S.fp_ok, a - 1)
                    for k in range(2):
                        ins = dve.tensor_scalar(h_t[:, b, k, :], tph[b][:, k, :], b1[:, k, bass.ds(e, 1)], 0.0,
                                                ALU.add, ALU.max)
                    ins.then_inc(S.h_t_ok, 1)
                if (a := stage(XT, t, LAG_F)) is not None:
                    b, j = (i - LAG_F) % 2, (i - LAG_F) % U
                    e = dve.value_load(lots[0:1, 0, bass.ds(a, 1)], min_val=0, max_val=EXPERTS - 1)
                    dve.wait_ge(S.fp_ok, a + 1)
                    wait_past(dve, S.out_ok, a)
                    dve.tensor_tensor(f[:, :], fp[b][:, :], flat(b2[:, bass.ds(e, 1), :]), ALU.add).then_inc(S.f_ok, 1)
                    dve.wait_ge(S.f_ok, a + 1)
                    if not (isinstance(a, int) and a < U):
                        dve.wait_ge(out_st[j], 16 * (turns(a, j) - 1))
                    dve.scalar_tensor_tensor(out=out[:, j, :], in0=f[:, :], scalar=score[:, j:j + 1],
                                             in1=rows[:, j, 0:DIM], op0=ALU.mult, op1=ALU.add).then_inc(S.out_ok, 1)

            in_turn(dve, XT, U, LAG_F, body)


def program(nc, D):
    with ExitStack() as ctx:
        m = Memory(nc, ctx, "all")
        K = Names()
        K.g_in = m.sems("g_in", RING)
        K.ids_st = m.sem("ids_st")
        K.rows_in = m.sems("rows_in", UNROLL)
        K.out_st = m.sems("out_st", UNROLL)
        K.ident = m.sb("ident", [P, P])
        K.upper = m.sb("upper", [P, P])
        K.ones = m.sb("ones", [P, P])
        K.ident16 = m.sb("ident16", [P, P], F16)
        K.iota16 = m.sb("iota16", [P, P], F16)
        K.ones16 = m.sb("ones16", [P, 1], F16)
        K.pos = m.sb("pos", [P, 512])
        K.part = m.sb("part", [P, G_BLOCKS])
        K.base = m.sb("base", [P, TILES])
        K.pad_bias = m.sb("pad_bias", [P, TILES])
        K.rq = m.sb("rq", [P, TILES])
        K.deg = m.sb("deg", [P, TILES])
        K.context = m.sb("context", [P, PAIRS, P + 1])
        K.m_old = m.sb("m_old", [P, PAIRS])
        K.run = m.sb("run", [P, EXPERTS])
        K.node = m.sb("node", [P, 1])
        K.scratch = m.sb("scratch", [P, 64])
        acc_held = ctx.enter_context(ExitStack())
        K.acc = Memory(nc, acc_held, "held").sb("acc", [P, TILES, DIM])
        with ExitStack() as early:
            m2 = Memory(nc, early, "early")
            K.src, K.dst = m2.sb("src_cols", [P, EDGE_COLS], I16), m2.sb("dst_cols", [P, EDGE_COLS])
            K.ent = m2.sb("ent", [1, 2, ENTRIES + 7], I32)
            K.rounds = m2.sb("rounds", [1, 1], I32)
            K.gfirst, K.gstart, K.gend = (m2.sb(n, [G_PART, G_BLOCKS]) for n in ("gfirst", "gstart", "gend"))
            K.lhs = m2.sb("lhs", [G_PART, 3, G_BLOCKS])
            K.kmax = m2.sb("kmax", [P, DIM])
            K.wq_hi, K.wq_lo = m2.sb("wq_hi", [P, KC, 3 * DIM], F16), m2.sb("wq_lo", [P, KC, 3 * DIM], F16)
            normalize(nc, K, D)
            aggregate(nc, K, D)
            further = nc.values_load(K.rounds[0:1, 0:1], min_val=0, max_val=ROUNDS)
            with nc.If(further > 0):
                with nc.Fori(0, further):
                    next_round(nc, K, D)
            nc.all_engine_barrier()
        with ExitStack() as late:
            m2 = Memory(nc, late, "late")
            K.wn_hi, K.wn_lo = m2.sb("wn_hi", [P, 2, KC, DIM], F16), m2.sb("wn_lo", [P, 2, KC, DIM], F16)
            K.c2, K.vec = m2.sb("c2", [P, PAIRS, DIM]), m2.sb("vec", [P, 4, DIM])
            K.wg, K.bg, K.falling = m2.sb("wg", [P, KC, EXPERTS]), m2.sb("bg", [P, EXPERTS]), m2.sb("falling", [P, EXPERTS])
            K.unscale = m2.sb("unscale", [P, 1])
            fold(nc, K, D)
            mix(nc, K, D)
        acc_held.close()
        experts(nc, K, D)


def lay_out(a):
    def rows(w):
        return np.ascontiguousarray(w.reshape(-1, P, w.shape[-1]).transpose(1, 0, 2))

    x = np.zeros((ROWS, DIM), np.float32)
    x[:N_NODES] = a["x"]
    edges = (GROUPS + 1) * GROUP * P
    src = np.zeros(edges, np.int32)
    src[:N_EDGES] = a["src"]
    dst = np.full(edges, -1, np.int32)
    dst[:GROUPS * GROUP * P] = ROWS - 1
    dst[:N_EDGES] = a["dst"]
    return {
        "x": x,
        "src": np.ascontiguousarray(src.reshape(-1, P).T),
        "dst": np.ascontiguousarray(dst.reshape(-1, P).T),
        "dst_groups": np.ascontiguousarray(dst[:GROUPS * GROUP * P].reshape(G_BLOCKS, G_PART, GROUP * P).transpose(1, 0, 2)),
        "wqkv": rows(a["L0_mix_w_qkv"].T),
        "w_self": rows(a["L0_gnn_W_self"].T),
        "w_neigh": rows(a["L0_gnn_W_neigh"].T),
        "w_out": rows(a["L0_mix_w_out"].T),
        "bias": a["L0_gnn_bias"].reshape(1, -1),
        "gamma": a["L0_gnn_gamma"].reshape(1, -1),
        "beta": a["L0_gnn_beta"].reshape(1, -1),
        "out_gamma": a["L0_mix_out_gamma"].reshape(1, -1),
        "w_gate": rows(a["L0_ffn_Wg"]),
        "b_gate": a["L0_ffn_bg"].reshape(1, -1),
        "w1": np.ascontiguousarray(a["L0_ffn_W1"].reshape(EXPERTS, KC, P, HIDDEN).transpose(2, 0, 1, 3)),
        "w2": np.ascontiguousarray(a["L0_ffn_W2"].reshape(EXPERTS, 2, P, DIM).transpose(2, 0, 1, 3)),
        "b1": np.ascontiguousarray(a["L0_ffn_b1"].reshape(EXPERTS, 2, P).transpose(2, 1, 0)),
        "b2": a["L0_ffn_b2"].reshape(1, -1),
        "norm_gamma": np.ascontiguousarray(a["L0_mix_norm_gamma"].reshape(KC, P).T),
    }


def kernel(**inputs):
    import concourse.bacc as bacc
    from concourse.bass_utils import run_bass_kernel_spmd as run

    arrays = lay_out({k: np.asarray(v) for k, v in inputs.items()})
    nc = bacc.Bacc("TRN2", target_bir_lowering=False, num_devices=1)
    D = {k: nc.dram_tensor(f"in_{k}", v.shape, mybir.dt.from_np(v.dtype), kind="ExternalInput").ap()
         for k, v in arrays.items()}
    for k, s, d in (("table", (ROWS, 2 * DIM), F16), ("q", (ROWS, DIM), F32), ("perm", (EXPERTS * BUCKET + P, 1), I32),
                    ("x1", (ROWS, X1W), F32)):
        D[k] = nc.dram_tensor(f"dram_{k}", s, d, kind="Internal").ap()
    D["out"] = nc.dram_tensor("out", (ROWS, DIM), F32, kind="ExternalOutput").ap()
    program(nc, D)
    r = run(nc, [{f"in_{k}": v for k, v in arrays.items()}], core_ids=[0])
    return r.results[0]["out"][:N_NODES]
```

```python
from contextlib import ExitStack

import numpy as np

import concourse.bass as bass
import concourse.mybir as mybir

F32, F16, I32 = mybir.dt.float32, mybir.dt.float16, mybir.dt.int32
ALU = mybir.AluOpType
ACT = mybir.ActivationFunctionType
AX = mybir.AxisListType
MAX_ALL = bass.bass_isa.ReduceOp.max

P = 128
N_NODES, DIM = 6250, 512
N_EDGES = 100000
HEADS, HEAD_DIM = 8, 64
PAIRS = HEADS // 2
EXPERTS, HIDDEN = 8, 256
EPS = 1e-5
TILES = -(-N_NODES // P)
ROWS = TILES * P
CHUNK = 7
CHUNKS = TILES // CHUNK
KC = DIM // P
GROUP = 2
GROUPS = -(-N_EDGES // (GROUP * P)) + 1
PACK = 3
G_PART = 98
G_BLOCKS = GROUPS // G_PART
ENTRIES = 441
PER_CHUNK = ENTRIES // CHUNKS
PIECE = 9
PER_STEP = 8
RING = 7
AHEAD = 3
XS = 2048.0
BIG = 1e30
X1W = 528
BUCKET = ROWS
XT = ROWS // P + EXPERTS - 1
UNROLL = 8
ROUNDS = 44

assert CHUNKS * CHUNK == TILES and G_PART * G_BLOCKS == GROUPS and PER_CHUNK * CHUNKS == ENTRIES
assert GROUPS + TILES - 1 <= ENTRIES


class Names:
    pass


class Memory:

    def __init__(self, nc, ctx, stage):
        self.nc, self.ctx, self.stage, self.named = nc, ctx, stage, []
        ctx.callback(self.clear)

    def clear(self):
        if self.named:
            self.nc.clear_and_free_semaphores(self.named)
            self.nc.all_engine_barrier()

    def sb(self, name, shape, dtype=F32):
        return self.ctx.enter_context(self.nc.sbuf_tensor(f"{self.stage}_{name}", shape, dtype))

    def ps(self, name, shape, dtype=F32):
        return self.ctx.enter_context(self.nc.psum_tensor(f"{self.stage}_{name}", shape, dtype))

    def sem(self, name):
        self.named.append(self.nc.alloc_semaphore(name=f"{self.stage}_{name}"))
        return self.named[-1]

    def sems(self, name, n):
        return [self.sem(f"{name}{i}") for i in range(n)]


def flat(ap):
    return ap.rearrange("p a b -> p (a b)")


def bcast(ap, n):
    return ap.unsqueeze(2).to_broadcast([ap.shape[0], ap.shape[1], n])


def wait_past(eng, sem, count):
    if not (isinstance(count, int) and count <= 0):
        eng.wait_ge(sem, count)


def chunks(eng, body):
    body(0)
    with eng.Fori(1, CHUNKS) as c:
        body(c)


def in_turn(eng, total, unroll, lag, body):
    for t in range(unroll):
        body(t, t)
    with eng.Fori(1, total // unroll) as c:
        for i in range(unroll):
            body(unroll * c + i, i)
    for t in range(total, total + lag):
        body(t, t % unroll)


def stage(total, t, lag):
    at = t - lag
    return at if not isinstance(t, int) or 0 <= at < total else None


class Chain:

    def __init__(self, eng, sem, n, t):
        self.eng, self.sem, self.n, self.t, self.k = eng, sem, n, t, 0

    def __call__(self, ins):
        self.k += 1
        assert self.k <= self.n
        ins.then_inc(self.sem, 1)
        self.eng.wait_ge(self.sem, self.n * self.t + self.k)


def power_of_two(dve, link, out, biggest, one_over, tmp_i):
    link(dve.tensor_scalar(out, biggest, 1e-30, None, ALU.max))
    link(dve.tensor_scalar(tmp_i, out.bitcast(I32), 0x7F800000, None, ALU.bitwise_and))
    link(dve.tensor_scalar(one_over, tmp_i.bitcast(F32), 2.0 ** -14, None, ALU.mult))
    link(dve.reciprocal(out, one_over))


def entry_memory(m):
    T = Names()
    T.dst, T.src = m.sb("dst_i", [G_PART, G_BLOCKS, GROUP * P], I32), m.sb("src_i", [G_PART, G_BLOCKS, GROUP * P], I32)
    T.dst_f, T.src_f = T.dst[:, :, :].bitcast(F32), T.src[:, :, :].bitcast(F32)
    T.begun, T.holds = m.sb("begun", [G_PART, ENTRIES]), m.sb("holds", [G_PART, G_BLOCKS, ENTRIES])
    T.off, T.lhs = m.sb("off", [G_PART, G_BLOCKS]), m.sb("lhs", [G_PART, 2, G_BLOCKS])
    T.wrow, T.pack = m.sb("wrow", [1, ENTRIES]), m.sb("pack", [1, ENTRIES // PACK])
    T.nodes = [m.ps(f"nodes{i}", [P, 512]) for i in range(2 * GROUP)]
    T.wins = [m.ps(f"wins{i}", [1, 512]) for i in range(2)]
    return T


def entry_groups(dve, link, K, T):
    link(dve.tensor_tensor(T.lhs[:, 0, :], K.gfirst[:, :], K.gstart[:, :], ALU.subtract))
    link(dve.memset(T.lhs[:, 1, :], 1.0))
    link(dve.tensor_scalar(T.off[:, :], T.lhs[:, 0, :], float(P), None, ALU.mult))
    link(dve.tensor_copy(flat(T.src_f[:, :, :]), flat(T.src[:, :, :])))
    link(dve.tensor_copy(flat(T.dst_f[:, :, :]), flat(T.dst[:, :, :])))
    for b in range(G_BLOCKS):
        link(dve.tensor_scalar(T.dst_f[:, b, :], T.dst_f[:, b, :], T.off[:, b:b + 1], None, ALU.subtract))
        link(dve.tensor_scalar(T.begun[:, :], K.pos[0:G_PART, 0:ENTRIES], K.gstart[:, b:b + 1], None, ALU.is_ge))
        ins = dve.scalar_tensor_tensor(out=T.holds[:, b, :], in0=K.pos[0:G_PART, 0:ENTRIES],
                                       scalar=K.gend[:, b:b + 1], in1=T.begun[:, :], op0=ALU.is_lt, op1=ALU.mult)
        if b < G_BLOCKS - 1:
            link(ins)
    return ins


def entry_sums(pe, T):
    for r in range(2):
        for b in range(G_BLOCKS):
            pe.matmul(T.wins[r][:, 0:ENTRIES], T.lhs[:, r, b:b + 1], T.holds[:, b, :],
                      start=(b == 0), stop=(b == G_BLOCKS - 1))
    for r, values in enumerate((T.dst_f, T.src_f)):
        for u in range(GROUP):
            for b in range(G_BLOCKS):
                mm = pe.matmul(T.nodes[GROUP * r + u][:, 0:ENTRIES], values[:, b, u * P:(u + 1) * P], T.holds[:, b, :],
                               start=(b == 0), stop=(b == G_BLOCKS - 1))
    return mm


def entry_values(dve, link, K, T):
    link(dve.tensor_tensor(T.wrow[:, :], T.wins[1][:, 0:ENTRIES], K.pos[0:1, 0:ENTRIES], ALU.mult))
    link(dve.tensor_tensor(T.wrow[:, :], T.wins[0][:, 0:ENTRIES], T.wrow[:, :], ALU.add))
    by = T.wrow[:, :].rearrange("p (a b) -> p a b", b=PACK)
    link(dve.scalar_tensor_tensor(out=T.pack[:, :], in0=by[:, :, 2], scalar=64.0, in1=by[:, :, 1],
                                  op0=ALU.mult, op1=ALU.add))
    link(dve.scalar_tensor_tensor(out=T.pack[:, :], in0=T.pack[:, :], scalar=64.0, in1=by[:, :, 0],
                                  op0=ALU.mult, op1=ALU.add))
    link(dve.tensor_copy(K.packs[:, :], T.pack[:, :]))
    for u in range(GROUP):
        link(dve.scalar_tensor_tensor(out=K.rel[:, u, 0:ENTRIES], in0=K.pos[:, 0:ENTRIES], scalar=-float(P),
                                      in1=T.nodes[u][:, 0:ENTRIES], op0=ALU.mult, op1=ALU.add))
        link(dve.tensor_copy(K.idx[:, :, u], T.nodes[GROUP + u][:, 0:ENTRIES]))


def windows(dve, K, m):
    word = dve.value_load(K.packs[0:1, bass.ds(m, 1)], min_val=0, max_val=64 ** PACK - 1)
    return [((word >> (6 * i)) & 63).with_bounds(min_val=0, max_val=TILES - 1) for i in range(PACK)]


def normalize(nc, K, D):
    with ExitStack() as ctx:
        m = Memory(nc, ctx, "normalize")
        x = m.sb("x", [P, 2, CHUNK, DIM])
        halves = m.sb("halves", [P, CHUNK, 2, DIM], F16)
        stats = m.sb("stats", [P, CHUNK, 6])
        mv = m.sb("mv", [P, CHUNK, 2])
        sd = m.sb("sd", [P, CHUNK])
        veps = m.sb("veps", [P, CHUNK])
        scale = m.sb("scale", [P, 2, CHUNK])
        shift = m.sb("shift", [P, 2, CHUNK])
        var_all = m.sb("var_all", [P, TILES])
        inv_all = m.sb("inv_all", [P, TILES])
        sd_all = m.sb("sd_all", [P, TILES])
        staged = 3 * KC
        wq = flat(K.acc[:, 0:staged, :]).rearrange("p (a b) -> p a b", a=KC)
        gam = m.sb("gam", [P, KC])
        wmax = m.sb("wmax", [P, 1])
        wall = m.sb("wall", [P, 1])
        wscale = m.sb("wscale", [P, 1])
        wbits = m.sb("wbits", [P, 1], I32)
        unscale = m.sb("unscale", [P, 1])
        T = entry_memory(m)
        gwin = m.sb("gwin", [G_PART, 2, G_BLOCKS], I32)
        gcount = m.sb("gcount", [G_PART, G_BLOCKS])
        glast = m.sb("glast", [G_PART, G_BLOCKS])
        before = m.sb("before", [G_PART, G_BLOCKS])
        more, rounds_f = m.sb("more", [1, ROUNDS]), m.sb("rounds_f", [1, 1])
        oob = m.sb("oob", [P, (EXPERTS * BUCKET + P) // P], I32)
        psum_c = m.ps("psum_c", [P, 512])
        x_in, stored = m.sems("x_in", 2 * CHUNK), m.sems("stored", CHUNK)
        w_in, e_in, oob_st = m.sem("w_in"), m.sem("e_in"), m.sem("oob_st")
        xn_ok, stat_ok, mv_ok, veps_ok, sd_ok, inv_ok, scale_ok = (m.sem(s) for s in (
            "xn_ok", "stat_ok", "mv_ok", "veps_ok", "sd_ok", "inv_ok", "scale_ok"))
        hi_ok, lo_ok = m.sem("hi_ok"), m.sem("lo_ok")
        made, link_ok, wmax_ok, wall_ok = m.sem("made"), m.sem("link_ok"), m.sem("wmax_ok"), m.sem("wall_ok")
        split_ok, spare = m.sem("split_ok"), m.sem("spare")
        cnt_ok, prefix_ok, holds_ok, ent_ok = m.sem("cnt_ok"), m.sem("prefix_ok"), m.sem("holds_ok"), m.sem("ent_ok")
        var2_ok, sd2_ok = m.sem("var2_ok"), m.sem("sd2_ok")
        block = ctx.enter_context(nc.Block())

        @block.sync
        def _(sp):
            sp.dma_start(T.dst[:, :, :], D["dst"]).then_inc(e_in, 16)
            sp.dma_start(T.src[:, :, :], D["src"]).then_inc(e_in, 16)

            def load(c, b, i):
                sp.dma_start(x[:, b, i, :], D["x"][bass.ds((CHUNK * c + i) * P, P), :]).then_inc(x_in[CHUNK * b + i], 16)

            def store(c, i):
                sp.wait_ge(lo_ok, CHUNK * c + i + 1)
                sp.dma_start(D["table"][bass.ds((CHUNK * c + i) * P, P), :],
                             flat(halves[:, i, :, :])).then_inc(stored[i], 16)

            for i in range(CHUNK):
                load(0, 0, i)
            sp.dma_start(wq[:, :, :], D["wqkv"]).then_inc(w_in, 16)
            sp.dma_start(gam[:, :], D["norm_gamma"]).then_inc(w_in, 16)
            for i in range(CHUNK):
                load(1, 1, i)
            with sp.Fori(0, CHUNKS // 2 - 1) as j:
                for b in range(2):
                    for i in range(CHUNK):
                        store(2 * j + b, i)
                        load(2 * j + b + 2, b, i)
            for c in range(CHUNKS - 3, CHUNKS):
                for i in range(CHUNK):
                    store(c, i)
                    if c + 2 < CHUNKS:
                        load(c + 2, c % 2, i)
            sp.wait_ge(made, 6)
            sp.dma_start(D["perm"].rearrange("(p a) b -> p (a b)", p=P), oob[:, :]).then_inc(oob_st, 16)
            for i in range(CHUNK):
                sp.wait_ge(stored[i], 16 * CHUNKS)
            sp.wait_ge(oob_st, 16)

        @block.gpsimd
        def _(pool):
            pool.memset(K.ident[:, :], 0.0).then_inc(made, 1)
            pool.memset(K.upper[:, :], 1.0).then_inc(made, 1)
            pool.memset(K.ones[:, :], 1.0).then_inc(made, 1)
            pool.memset(K.pad_bias[:, :], 0.0).then_inc(made, 1)
            pool.memset(oob[:, :], ROWS).then_inc(made, 1)
            pool.iota(K.pos[:, :], [[1, 512]], base=0, channel_multiplier=0,
                      allow_small_or_imprecise_dtypes=True).then_inc(made, 1)
            pool.wait_ge(made, 6)
            pool.affine_select(out=K.ident[:, :], in_=K.ident[:, :], compare_op=ALU.not_equal, fill=1.0, base=0,
                               pattern=[[-1, P]], channel_multiplier=1).then_inc(made, 1)
            pool.affine_select(out=K.upper[:, :], in_=K.upper[:, :], compare_op=ALU.is_gt, fill=0.0, base=0,
                               pattern=[[1, P]], channel_multiplier=-1).then_inc(made, 1)
            pool.affine_select(out=K.pad_bias[:, :], in_=K.pad_bias[:, :], compare_op=ALU.is_gt, fill=-BIG,
                               base=N_NODES, pattern=[[-P, TILES]], channel_multiplier=-1).then_inc(made, 1)
            pool.iota(K.node[:, :], [[0, 1]], base=0, channel_multiplier=1,
                      allow_small_or_imprecise_dtypes=True).then_inc(made, 1)
            pool.memset(K.deg[:, :], 0.0).then_inc(made, 1)
            pool.memset(K.kmax[:, :], -BIG).then_inc(made, 1)
            pool.memset(K.m_old[:, :], -BIG).then_inc(made, 1)
            pool.memset(K.context[:, :, :], 0.0).then_inc(made, 1)
            pool.wait_ge(wmax_ok, 1)
            pool.partition_all_reduce(wall[:, :], wmax[:, :], P, MAX_ALL).then_inc(wall_ok, 1)
            for t in range(staged, TILES):
                pool.memset(K.acc[:, t, :], 0.0).then_inc(made, 1)
            pool.wait_ge(split_ok, 1)
            for t in range(staged):
                pool.memset(K.acc[:, t, :], 0.0).then_inc(made, 1)

        @block.scalar
        def _(act):
            def tiles(c, b):
                act.wait_ge(veps_ok, c + 1)
                act.activation(sd[:, :], veps[:, :], ACT.Sqrt).then_inc(sd_ok, 1)
                act.wait_ge(scale_ok, c + 1)
                for i in range(CHUNK):
                    act.activation(x[:, b, i, :], x[:, b, i, :], ACT.Identity, bias=shift[:, b, i:i + 1],
                                   scale=scale[:, b, i:i + 1]).then_inc(xn_ok, 1)
                    wait_past(act, stored[i], 16 * c)
                    act.wait_ge(xn_ok, CHUNK * c + i + 1)
                    act.copy(halves[:, i, 0, :], x[:, b, i, :]).then_inc(hi_ok, 1)

            tiles(0, 0)
            with act.Fori(0, CHUNKS // 2) as j:
                tiles(2 * j + 1, 1)
                tiles(2 * j + 2, 0)
            act.wait_ge(var2_ok, 1)
            act.activation(sd_all[:, :], inv_all[:, :], ACT.Sqrt).then_inc(sd2_ok, 1)

        @block.tensor
        def _(pe):
            pe.wait_ge(made, 9)
            pe.wait_ge(cnt_ok, 1)
            pe.matmul(psum_c[0:G_PART, 0:G_BLOCKS], K.upper[0:G_PART, 0:G_PART], gcount[:, :], start=True, stop=True)
            pe.matmul(psum_c[0:G_PART, G_BLOCKS:2 * G_BLOCKS], K.ones[0:G_PART, 0:G_PART], gcount[:, :],
                      start=True, stop=True).then_inc(prefix_ok, 1)
            pe.wait_ge(holds_ok, 1)
            mm = entry_sums(pe, T)
            mm.then_inc(ent_ok, 1)

        @block.vector
        def _(dve):
            done = [0]

            def link(ins):
                done[0] += 1
                ins.then_inc(link_ok, 1)
                dve.wait_ge(link_ok, done[0])

            def edges_first():
                dve.wait_ge(e_in, 32)
                dve.wait_ge(made, 9)
                link(dve.memset(K.rel[:, :, ENTRIES:], -1.0))
                link(dve.tensor_reduce(gwin[:, 0, :], T.dst[:, :, :], AX.X, ALU.min))
                link(dve.tensor_reduce(gwin[:, 1, :], T.dst[:, :, :], AX.X, ALU.max))
                link(dve.tensor_scalar(gwin[:, :, :], gwin[:, :, :], 7, None, ALU.arith_shift_right))
                link(dve.tensor_copy(K.gfirst[:, :], gwin[:, 0, :]))
                link(dve.tensor_copy(glast[:, :], gwin[:, 1, :]))
                link(dve.tensor_tensor(gcount[:, :], glast[:, :], K.gfirst[:, :], ALU.subtract))
                dve.tensor_scalar(gcount[:, :], gcount[:, :], 1.0, None, ALU.add).then_inc(cnt_ok, 1)
                dve.wait_ge(prefix_ok, 1)
                link(dve.memset(before[:, 0:1], 0.0))
                for b in range(1, G_BLOCKS):
                    link(dve.tensor_tensor(before[:, b:b + 1], before[:, b - 1:b],
                                           psum_c[0:G_PART, G_BLOCKS + b - 1:G_BLOCKS + b], ALU.add))
                link(dve.tensor_tensor(K.gstart[:, :], before[:, :], psum_c[0:G_PART, 0:G_BLOCKS], ALU.add))
                link(dve.tensor_tensor(K.gend[:, :], K.gstart[:, :], gcount[:, :], ALU.add))
                entry_groups(dve, link, K, T).then_inc(holds_ok, 1)

            def edges_last():
                dve.wait_ge(ent_ok, 1)
                entry_values(dve, link, K, T)
                link(dve.tensor_tensor(before[:, 0:1], before[:, G_BLOCKS - 1:G_BLOCKS],
                                       psum_c[0:G_PART, 2 * G_BLOCKS - 1:2 * G_BLOCKS], ALU.add))
                link(dve.tensor_scalar(more[:, :], K.pos[0:1, 1:ROUNDS + 1], float(ENTRIES), before[0:1, 0:1],
                                       ALU.mult, ALU.is_lt))
                link(dve.tensor_reduce(rounds_f[:, :], more[:, :], AX.X, ALU.add))
                link(dve.tensor_copy(K.rounds[:, :], rounds_f[:, :]))

            def weights_max():
                dve.wait_ge(w_in, 32)
                for k in range(KC):
                    link(dve.tensor_scalar(wq[:, k, :], wq[:, k, :], gam[:, k:k + 1], None, ALU.mult))
                dve.tensor_reduce(wmax[:, :], flat(wq[:, :, :]), AX.X, ALU.max,
                                  apply_absolute_value=True).then_inc(wmax_ok, 1)

            def weights_split():
                dve.wait_ge(wall_ok, 1)
                power_of_two(dve, link, wscale[:, :], wall[:, :], unscale[:, :], wbits[:, :])
                link(dve.tensor_scalar(flat(K.wq_hi[:, :, :]), flat(wq[:, :, :]), wscale[:, :], None, ALU.mult))
                dve.scalar_tensor_tensor(out=flat(K.wq_lo[:, :, :]), in0=flat(wq[:, :, :]), scalar=wscale[:, :],
                                         in1=flat(K.wq_hi[:, :, :]), op0=ALU.mult, op1=ALU.subtract).then_inc(split_ok, 1)

            def statistics(c, b, k):
                for i in range(CHUNK):
                    dve.wait_ge(x_in[CHUNK * b + i], 16 * (k + 1))
                    dve.bn_stats(stats[:, i, :], x[:, b, i, :]).then_inc(stat_ok, 1)
                dve.wait_ge(stat_ok, CHUNK * (c + 1))
                dve.sem_inc(spare, 1)
                for i in range(CHUNK):
                    dve.bn_aggr(mv[:, i, :], stats[:, i, :]).then_inc(mv_ok, 1)
                dve.wait_ge(mv_ok, CHUNK * (c + 1))
                dve.tensor_scalar(veps[:, :], mv[:, :, 1], EPS, None, ALU.add).then_inc(veps_ok, 1)
                dve.tensor_copy(var_all[:, bass.ds(CHUNK * c, CHUNK)], mv[:, :, 1])
                dve.wait_ge(sd_ok, c + 1)
                dve.reciprocal(inv_all[:, bass.ds(CHUNK * c, CHUNK)], sd[:, :]).then_inc(inv_ok, 1)
                dve.wait_ge(inv_ok, 3 * c + 1)
                dve.tensor_scalar(scale[:, b, :], inv_all[:, bass.ds(CHUNK * c, CHUNK)], XS, None,
                                  ALU.mult).then_inc(inv_ok, 1)
                dve.wait_ge(inv_ok, 3 * c + 2)
                dve.tensor_tensor(shift[:, b, :], mv[:, :, 0], scale[:, b, :], ALU.mult).then_inc(inv_ok, 1)
                dve.wait_ge(inv_ok, 3 * c + 3)
                dve.tensor_scalar(shift[:, b, :], shift[:, b, :], -1.0, None, ALU.mult).then_inc(scale_ok, 1)

            def low_halves(c, b):
                for i in range(CHUNK):
                    dve.wait_ge(hi_ok, CHUNK * c + i + 1)
                    dve.tensor_tensor(halves[:, i, 1, :], x[:, b, i, :], halves[:, i, 0, :],
                                      ALU.subtract).then_inc(lo_ok, 1)

            edges_first()
            statistics(0, 0, 0)
            weights_max()
            statistics(1, 1, 0)
            low_halves(0, 0)
            weights_split()
            edges_last()
            statistics(2, 0, 1)
            low_halves(1, 1)
            with dve.Fori(1, CHUNKS // 2) as j:
                statistics(2 * j + 1, 1, j)
                low_halves(2 * j, 0)
                statistics(2 * j + 2, 0, j + 1)
                low_halves(2 * j + 1, 1)
            low_halves(CHUNKS - 1, 0)
            link(dve.tensor_copy(K.scratch[:, 0:TILES], inv_all[:, :]))
            link(dve.tensor_tensor(inv_all[:, :], inv_all[:, :], K.scratch[:, 0:TILES], ALU.mult))
            link(dve.tensor_tensor(inv_all[:, :], inv_all[:, :], var_all[:, :], ALU.mult))
            dve.tensor_scalar(inv_all[:, :], inv_all[:, :], EPS, None, ALU.add).then_inc(var2_ok, 1)
            dve.wait_ge(sd2_ok, 1)
            link(dve.reciprocal(K.rq[:, :], sd_all[:, :]))
            link(dve.tensor_scalar(K.rq[:, :], K.rq[:, :], unscale[:, :], 1.0 / XS, ALU.mult, ALU.mult))
            link(dve.tensor_copy(K.ident16[:, :], K.ident[:, :]))
            link(dve.tensor_copy(K.iota16[:, :], K.pos[:, 0:P]))
            link(dve.tensor_copy(K.ones16[:, :], K.ones[:, 0:1]))


def aggregate(nc, K, D):
    with ExitStack() as ctx:
        m = Memory(nc, ctx, "aggregate")
        rows = m.sb("rows", [P, RING, GROUP, 2 * DIM], F16)
        picks = m.sb("picks", [P, RING, GROUP, P], F16)
        cols = m.sb("cols", [P, PER_CHUNK, GROUP], I32)
        xrow = m.sb("xrow", [P, 2 * KC, P], F16)
        x_t = m.sb("x_t", [P, 2 * KC, P], F16)
        q = m.sb("q", [P, HEADS, HEAD_DIM])
        q_exp = m.sb("q_exp", [P, HEADS, HEAD_DIM])
        q_top = m.sb("q_top", [P, HEADS])
        q_sum = m.sb("q_sum", [P, HEADS])
        kbuf = m.sb("kbuf", [P, CHUNK, DIM])
        vbuf = m.sb("vbuf", [P, CHUNK, PAIRS, P + 1])
        rq, pad_bias = m.sb("rq", [P, CHUNK]), m.sb("pad_bias", [P, CHUNK])
        rq_ok = m.sem("rq_ok")
        m_new = m.sb("m_new", [P, PAIRS])
        m_step = m.sb("m_step", [P, PAIRS])
        decay = m.sb("decay", [P, PAIRS])
        diag = flat(q_exp[:, :, :]).rearrange("p (a b) -> p a b", a=PAIRS)
        ag = [m.ps(f"ag{i}", [P, DIM]) for i in range(2)]
        dg = m.ps("dg", [P, 512])
        bank_a, bank_b = m.ps("bank_a", [P, DIM]), m.ps("bank_b", [P, DIM])
        tp = m.ps("tp", [P, 2 * KC, P], F16)
        ct = [m.ps(f"ct{i}", [P, 2, P + 1]) for i in range(2)]
        col_ok, picks_ok, ag_ok, acc_ok, deg_ok = (m.sem(s) for s in (
            "col_ok", "picks_ok", "ag_ok", "acc_ok", "deg_ok"))
        g_in = K.g_in
        spare = m.sem("spare")
        xr_in, tp_ok, xt_ok = m.sem("xr_in"), m.sem("tp_ok"), m.sem("xt_ok")
        q_ok, k_ok, v_ok = m.sem("q_ok"), m.sem("k_ok"), m.sem("v_ok")
        q_sub, q_exp_ok, q_chain, q_done, q_st = (m.sem(s) for s in ("q_sub", "q_exp_ok", "q_chain", "q_done", "q_st"))
        k_in, v_in, kmax_ok = m.sem("k_in"), m.sem("v_in"), m.sem("kmax_ok")
        ones_ok, kt_ok, m_chain, diag_ok, mb_ok = (m.sem(s) for s in ("ones_ok", "kt_ok", "m_chain", "diag_ok", "mb_ok"))
        decay_ok, k_less, k_exp, ct_ok, ct_done = (m.sem(s) for s in ("decay_ok", "k_less", "k_exp", "ct_ok", "ct_done"))
        block = ctx.enter_context(nc.Block())

        @block.sync
        def _(sp):
            def chunk(c):
                for i in range(CHUNK):
                    t = CHUNK * c + i
                    wait_past(sp, tp_ok, t)
                    sp.dma_start(flat(xrow[:, :, :]), D["table"][bass.ds(t * P, P), :]).then_inc(xr_in, 16)
                    if i > 0:
                        sp.wait_ge(q_done, t)
                        sp.dma_start(D["q"][bass.ds((t - 1) * P, P), :], flat(q[:, :, :])).then_inc(q_st, 16)
                sp.wait_ge(q_done, CHUNK * c + CHUNK)
                sp.dma_start(D["q"][bass.ds((CHUNK * c + CHUNK - 1) * P, P), :], flat(q[:, :, :])).then_inc(q_st, 16)

            chunks(sp, chunk)
            sp.wait_ge(q_st, 16 * TILES)

        @block.gpsimd
        def _(pool):
            pool.memset(vbuf[:, :, :, P:P + 1], 1.0).then_inc(ones_ok, 1)

            def chunk(c):
                for e in range(PER_CHUNK):
                    n, slot = PER_CHUNK * c + e, e % RING
                    wait_past(pool, ag_ok, n - RING + 1)
                    if e % PIECE == 0:
                        pool.tensor_copy(cols[:, e:e + PIECE, :], K.idx[:, bass.ds(n, PIECE), :]).then_inc(col_ok, 1)
                        pool.wait_ge(col_ok, PER_CHUNK // PIECE * c + e // PIECE + 1)
                    pool.sem_inc(spare, 1)
                    for u in range(GROUP):
                        pool.indirect_dma_start(rows[:, slot, u, :], None, D["table"],
                                                bass.IndirectOffsetOnAxis(ap=cols[:, e, u:u + 1], axis=0)
                                                ).then_inc(g_in[slot], 16)

            chunks(pool, chunk)

        @block.tensor
        def _(pe):
            def entry(c, e):
                n, slot = PER_CHUNK * c + e, e % RING
                pe.wait_ge(g_in[slot], 16 * GROUP * (PER_CHUNK // RING * c + e // RING + 1))
                pe.wait_ge(picks_ok, n + 1)
                wait_past(pe, acc_ok, n if e == 0 else n - 1)
                for u in range(GROUP):
                    for h in range(2):
                        pe.matmul(ag[e % 2][:, :], picks[:, slot, u, :], rows[:, slot, u, h * DIM:(h + 1) * DIM],
                                  start=(u == 0 and h == 0), stop=(u == GROUP - 1 and h == 1))
                wait_past(pe, deg_ok, n)
                for u in range(GROUP):
                    mm = pe.matmul(dg[:, e % 2:e % 2 + 1], picks[:, slot, u, :], K.ones16[:, :],
                                   start=(u == 0), stop=(u == GROUP - 1))
                mm.then_inc(ag_ok, 1)

            def project(bank, part):
                w = slice(part * DIM, (part + 1) * DIM)
                todo = [(a, b, k) for k in range(KC) for a, b in ((0, K.wq_hi), (0, K.wq_lo), (KC, K.wq_hi))]
                for j, (a, b, k) in enumerate(todo):
                    mm = pe.matmul(bank[:, :], x_t[:, a + k, :], b[:, k, w], start=(j == 0), stop=(j == len(todo) - 1))
                return mm

            def chunk(c):
                for i in range(CHUNK):
                    t, e0 = CHUNK * c + i, PER_STEP * i
                    pe.wait_ge(xr_in, 16 * (t + 1))
                    wait_past(pe, xt_ok, t)
                    for k in range(2 * KC):
                        mm = pe.transpose(tp[:, k, :], xrow[:, k, :], K.ident16[:, :])
                    mm.then_inc(tp_ok, 1)
                    entry(c, e0)
                    entry(c, e0 + 1)
                    pe.wait_ge(xt_ok, t + 1)
                    if i > 0:
                        pe.wait_ge(v_in, t)
                    else:
                        wait_past(pe, v_in, t)
                        wait_past(pe, m_chain, c * 3)
                    project(bank_a, 0).then_inc(q_ok, 1)
                    entry(c, e0 + 2)
                    entry(c, e0 + 3)
                    wait_past(pe, k_in, t)
                    if i == 0:
                        wait_past(pe, k_less, CHUNK * c)
                    project(bank_b, 1).then_inc(k_ok, 1)
                    entry(c, e0 + 4)
                    entry(c, e0 + 5)
                    pe.wait_ge(q_sub, t + 1)
                    project(bank_a, 2).then_inc(v_ok, 1)
                    entry(c, e0 + 6)
                    entry(c, e0 + 7)
                e1 = PER_STEP * CHUNK
                pe.wait_ge(kmax_ok, CHUNK * (c + 1))
                pe.wait_ge(v_in, CHUNK * (c + 1))
                for p in range(PAIRS):
                    mm = pe.transpose(bank_a[:, p * P:(p + 1) * P], K.kmax[:, p * P:(p + 1) * P], K.ident[:, :])
                mm.then_inc(kt_ok, 1)
                entry(c, e1)
                entry(c, e1 + 1)
                pe.wait_ge(diag_ok, c + 1)
                for p in range(PAIRS):
                    mm = pe.matmul(bank_b[:, p * P:(p + 1) * P], K.ones[:, :], diag[:, p, :], start=True, stop=True)
                mm.then_inc(mb_ok, 1)
                entry(c, e1 + 2)
                entry(c, e1 + 3)
                wait_past(pe, ct_done, c)
                for i in range(CHUNK):
                    pe.wait_ge(k_exp, CHUNK * c + i + 1)
                    for p in range(PAIRS):
                        mm = pe.matmul(ct[p // 2][:, p % 2, :], kbuf[:, i, p * P:(p + 1) * P], vbuf[:, i, p, :],
                                       start=(i == 0 and p % 2 == 0), stop=(i == CHUNK - 1), skip_group_check=True)
                    if i < 3:
                        entry(c, e1 + 4 + i)
                mm.then_inc(ct_ok, 1)

            pe.wait_ge(ones_ok, 1)
            chunks(pe, chunk)

        @block.scalar
        def _(act):
            def chunk(c):
                act.copy(rq[:, :], K.rq[:, bass.ds(CHUNK * c, CHUNK)]).then_inc(rq_ok, 1)
                act.copy(pad_bias[:, :], K.pad_bias[:, bass.ds(CHUNK * c, CHUNK)]).then_inc(rq_ok, 1)
                act.wait_ge(rq_ok, 2 * c + 2)
                for i in range(CHUNK):
                    t = CHUNK * c + i
                    act.wait_ge(tp_ok, t + 1)
                    wait_past(act, v_ok, t)
                    act.copy(x_t[:, :, :], tp[:, :, :]).then_inc(xt_ok, 1)
                    act.wait_ge(q_sub, t + 1)
                    act.activation(q_exp[:, :, :], q_exp[:, :, :], ACT.Exp, scale=rq[:, i:i + 1]).then_inc(q_exp_ok, 1)
                    act.wait_ge(k_ok, t + 1)
                    if i == 0:
                        wait_past(act, ct_ok, c)
                    act.activation(kbuf[:, i, :], bank_b[:, :], ACT.Identity, bias=pad_bias[:, i:i + 1],
                                   scale=rq[:, i:i + 1]).then_inc(k_in, 1)
                    act.wait_ge(v_ok, t + 1)
                    act.activation(vbuf[:, i, :, 0:P], bank_a[:, :].rearrange("p (a b) -> p a b", a=PAIRS), ACT.Copy,
                                   scale=rq[:, i:i + 1]).then_inc(v_in, 1)
                act.wait_ge(m_chain, 3 * c + 2)
                act.activation(decay[:, :], m_step[:, :], ACT.Exp).then_inc(decay_ok, 1)
                for i in range(CHUNK):
                    act.wait_ge(k_less, CHUNK * c + i + 1)
                    act.activation(kbuf[:, i, :], kbuf[:, i, :], ACT.Exp).then_inc(k_exp, 1)

            chunks(act, chunk)

        @block.vector
        def _(dve):
            def pick(c, e):
                n, slot = PER_CHUNK * c + e, e % RING
                wait_past(dve, ag_ok, n - RING + 1)
                for u in range(GROUP):
                    ins = dve.tensor_scalar(picks[:, slot, u, :], K.iota16[:, :], K.rel[:, u, bass.ds(n, 1)],
                                            None, ALU.is_equal)
                ins.then_inc(picks_ok, 1)

            def take(c, e):
                n = PER_CHUNK * c + e
                if e % PACK == 0:
                    wins[:] = windows(dve, K, PER_CHUNK // PACK * c + e // PACK)
                win = wins[e % PACK]
                wait_past(dve, acc_ok, n)
                dve.wait_ge(ag_ok, n + 1)
                deg = K.deg[:, bass.ds(win, 1)]
                dve.tensor_tensor(deg, deg, dg[:, e % 2:e % 2 + 1], ALU.add).then_inc(deg_ok, 1)
                acc = flat(K.acc[:, bass.ds(win, 1), :])
                dve.tensor_tensor(acc, acc, ag[e % 2][:, :], ALU.add).then_inc(acc_ok, 1)
                if e + AHEAD < PER_CHUNK:
                    pick(c, e + AHEAD)
                else:
                    pick(c + 1, e + AHEAD - PER_CHUNK)

            def chunk(c):
                for i in range(CHUNK):
                    t, e0 = CHUNK * c + i, PER_STEP * i
                    for e in range(3):
                        take(c, e0 + e)
                    dve.wait_ge(q_ok, t + 1)
                    q_ps = bank_a[:, :].rearrange("p (a b) -> p a b", a=HEADS)
                    dve.tensor_reduce(q_top[:, :], q_ps, AX.X, ALU.max).then_inc(q_chain, 1)
                    dve.wait_ge(q_chain, 3 * t + 1)
                    dve.tensor_tensor(q_exp[:, :, :], q_ps, bcast(q_top[:, :], HEAD_DIM), ALU.subtract).then_inc(q_sub, 1)
                    take(c, e0 + 3)
                    take(c, e0 + 4)
                    dve.wait_ge(q_exp_ok, t + 1)
                    dve.tensor_reduce(q_sum[:, :], q_exp[:, :, :], AX.X, ALU.add).then_inc(q_chain, 1)
                    dve.wait_ge(q_chain, 3 * t + 2)
                    dve.reciprocal(q_sum[:, :], q_sum[:, :]).then_inc(q_chain, 1)
                    dve.wait_ge(q_chain, 3 * t + 3)
                    wait_past(dve, q_st, 16 * t)
                    dve.tensor_tensor(q[:, :, :], q_exp[:, :, :], bcast(q_sum[:, :], HEAD_DIM), ALU.mult).then_inc(q_done, 1)
                    take(c, e0 + 5)
                    dve.wait_ge(k_in, t + 1)
                    wait_past(dve, kmax_ok, t)
                    dve.tensor_tensor(K.kmax[:, :], K.kmax[:, :], kbuf[:, i, :], ALU.max).then_inc(kmax_ok, 1)
                    take(c, e0 + 6)
                    take(c, e0 + 7)
                e1 = PER_STEP * CHUNK
                dve.wait_ge(kt_ok, c + 1)
                dve.tensor_reduce(m_new[:, :], bank_a[:, :].rearrange("p (a b) -> p a b", a=PAIRS), AX.X,
                                  ALU.max).then_inc(m_chain, 1)
                dve.wait_ge(m_chain, 3 * c + 1)
                dve.tensor_tensor(m_step[:, :], K.m_old[:, :], m_new[:, :], ALU.subtract).then_inc(m_chain, 1)
                dve.wait_ge(m_chain, 3 * c + 2)
                dve.tensor_copy(K.m_old[:, :], m_new[:, :]).then_inc(m_chain, 1)
                dve.wait_ge(q_done, CHUNK * (c + 1))
                for p in range(PAIRS):
                    ins = dve.tensor_scalar(diag[:, p, :], K.ident[:, :], m_new[:, p:p + 1], None, ALU.mult)
                ins.then_inc(diag_ok, 1)
                for e in range(3):
                    take(c, e1 + e)
                dve.wait_ge(mb_ok, c + 1)
                for i in range(CHUNK):
                    dve.tensor_tensor(kbuf[:, i, :], kbuf[:, i, :], bank_b[:, :], ALU.subtract).then_inc(k_less, 1)
                    if i < 4:
                        take(c, e1 + 3 + i)
                dve.wait_ge(decay_ok, c + 1)
                dve.wait_ge(ct_ok, c + 1)
                for p in range(PAIRS):
                    ins = dve.scalar_tensor_tensor(out=K.context[:, p, :], in0=K.context[:, p, :],
                                                   scalar=decay[:, p:p + 1], in1=ct[p // 2][:, p % 2, :],
                                                   op0=ALU.mult, op1=ALU.add)
                ins.then_inc(ct_done, 1)

            wins = []
            for e in range(AHEAD):
                pick(0, e)
            chunks(dve, chunk)


def next_round(nc, K, D):
    with ExitStack() as ctx:
        m = Memory(nc, ctx, "list")
        T = entry_memory(m)
        e_in, link_ok, holds_ok, ent_ok = m.sem("e_in"), m.sem("link_ok"), m.sem("holds_ok"), m.sem("ent_ok")
        block = ctx.enter_context(nc.Block())

        @block.sync
        def _(sp):
            sp.dma_start(T.dst[:, :, :], D["dst"]).then_inc(e_in, 16)
            sp.dma_start(T.src[:, :, :], D["src"]).then_inc(e_in, 16)

        @block.tensor
        def _(pe):
            pe.wait_ge(holds_ok, 1)
            entry_sums(pe, T).then_inc(ent_ok, 1)

        @block.vector
        def _(dve):
            done = [0]

            def link(ins):
                done[0] += 1
                ins.then_inc(link_ok, 1)
                dve.wait_ge(link_ok, done[0])

            link(dve.tensor_scalar(K.gstart[:, :], K.gstart[:, :], -float(ENTRIES), None, ALU.add))
            link(dve.tensor_scalar(K.gend[:, :], K.gend[:, :], -float(ENTRIES), None, ALU.add))
            dve.wait_ge(e_in, 32)
            entry_groups(dve, link, K, T).then_inc(holds_ok, 1)
            dve.wait_ge(ent_ok, 1)
            entry_values(dve, link, K, T)

    with ExitStack() as ctx:
        m = Memory(nc, ctx, "further")
        rows, picks = m.sb("rows", [P, GROUP, 2 * DIM], F16), m.sb("picks", [P, GROUP, P], F16)
        cols = m.sb("cols", [P, GROUP], I32)
        ag, dg = m.ps("ag", [P, DIM]), m.ps("dg", [P, 512])
        g_in, col_ok, picks_ok, ag_ok, acc_ok, spare = (m.sem(s) for s in (
            "g_in", "col_ok", "picks_ok", "ag_ok", "acc_ok", "spare"))
        block = ctx.enter_context(nc.Block())

        @block.gpsimd
        def _(pool):
            def entry(n):
                wait_past(pool, ag_ok, n)
                pool.tensor_copy(cols[:, :], flat(K.idx[:, bass.ds(n, 1), :])).then_inc(col_ok, 1)
                pool.wait_ge(col_ok, n + 1)
                pool.sem_inc(spare, 1)
                for u in range(GROUP):
                    pool.indirect_dma_start(rows[:, u, :], None, D["table"],
                                            bass.IndirectOffsetOnAxis(ap=cols[:, u:u + 1], axis=0)).then_inc(g_in, 16)

            entry(0)
            with pool.Fori(1, ENTRIES) as n:
                entry(n)

        @block.tensor
        def _(pe):
            def entry(n):
                pe.wait_ge(g_in, 16 * GROUP * (n + 1))
                pe.wait_ge(picks_ok, n + 1)
                wait_past(pe, acc_ok, n)
                for u in range(GROUP):
                    for h in range(2):
                        pe.matmul(ag[:, :], picks[:, u, :], rows[:, u, h * DIM:(h + 1) * DIM],
                                  start=(u == 0 and h == 0), stop=(u == GROUP - 1 and h == 1))
                for u in range(GROUP):
                    mm = pe.matmul(dg[:, 0:1], picks[:, u, :], K.ones16[:, :], start=(u == 0), stop=(u == GROUP - 1))
                mm.then_inc(ag_ok, 1)

            entry(0)
            with pe.Fori(1, ENTRIES) as n:
                entry(n)

        @block.vector
        def _(dve):
            def entry(n, win):
                wait_past(dve, acc_ok, n)
                for u in range(GROUP):
                    ins = dve.tensor_scalar(picks[:, u, :], K.iota16[:, :], K.rel[:, u, bass.ds(n, 1)], None,
                                            ALU.is_equal)
                ins.then_inc(picks_ok, 1)
                dve.wait_ge(ag_ok, n + 1)
                acc = flat(K.acc[:, bass.ds(win, 1), :])
                dve.tensor_tensor(acc, acc, ag[:, :], ALU.add)
                deg = K.deg[:, bass.ds(win, 1)]
                dve.tensor_tensor(deg, deg, dg[:, 0:1], ALU.add).then_inc(acc_ok, 1)

            def pack(m):
                for i, win in enumerate(windows(dve, K, m)):
                    entry(PACK * m + i, win)

            pack(0)
            with dve.Fori(1, ENTRIES // PACK) as m:
                pack(m)


def fold(nc, K, D):
    with ExitStack() as ctx:
        m = Memory(nc, ctx, "fold")
        w32 = m.sb("w32", [P, 2, KC, DIM])
        wo = m.sb("wo", [P, KC, DIM])
        wmax, wall, wscale = m.sb("wmax", [P, 1]), m.sb("wall", [P, 1]), m.sb("wscale", [P, 1])
        wbits = m.sb("wbits", [P, 1], I32)
        k_inv = m.sb("k_inv", [P, PAIRS])
        heads = m.sb("heads", [P, PAIRS, P])
        heads_t = m.sb("heads_t", [P, PAIRS, P])
        tp = m.ps("tp", [P, PAIRS, P])
        c2 = [m.ps(f"c2_{i}", [P, DIM]) for i in range(PAIRS)]
        w_in, o_in, v_in = m.sem("w_in"), m.sem("o_in"), m.sem("v_in")
        link_ok, wmax_ok, wall_ok = m.sem("link_ok"), m.sem("wmax_ok"), m.sem("wall_ok")
        heads_ok, tp_ok, heads_t_ok, c2_ok, c2_in = (m.sem(s) for s in ("heads_ok", "tp_ok", "heads_t_ok", "c2_ok", "c2_in"))
        block = ctx.enter_context(nc.Block())

        @block.sync
        def _(sp):
            sp.dma_start(w32[:, 0, :, :], D["w_self"]).then_inc(w_in, 16)
            sp.dma_start(w32[:, 1, :, :], D["w_neigh"]).then_inc(w_in, 16)
            sp.dma_start(wo[:, :, :], D["w_out"]).then_inc(o_in, 16)
            for i, name in enumerate(("bias", "gamma", "beta", "out_gamma")):
                sp.dma_start(K.vec[:, i, :], D[name].to_broadcast([P, DIM])).then_inc(v_in, 16)
            sp.dma_start(K.wg[:, :, :], D["w_gate"]).then_inc(v_in, 16)
            sp.dma_start(K.bg[:, :], D["b_gate"].to_broadcast([P, EXPERTS])).then_inc(v_in, 16)
            sp.wait_ge(v_in, 96)

        @block.gpsimd
        def _(pool):
            pool.wait_ge(wmax_ok, 1)
            pool.partition_all_reduce(wall[:, :], wmax[:, :], P, MAX_ALL).then_inc(wall_ok, 1)

        @block.tensor
        def _(pe):
            pe.wait_ge(heads_ok, 1)
            for p in range(PAIRS):
                mm = pe.transpose(tp[:, p, :], heads[:, p, :], K.ident[:, :])
            mm.then_inc(tp_ok, 1)
            pe.wait_ge(heads_t_ok, 1)
            pe.wait_ge(o_in, 16)
            for p in range(PAIRS):
                mm = pe.matmul(c2[p][:, :], heads_t[:, p, :], wo[:, p, :], start=True, stop=True)
            mm.then_inc(c2_ok, 1)

        @block.scalar
        def _(act):
            act.wait_ge(tp_ok, 1)
            act.copy(heads_t[:, :, :], tp[:, :, :]).then_inc(heads_t_ok, 1)
            act.wait_ge(c2_ok, 1)
            for p in range(PAIRS):
                act.copy(K.c2[:, p, :], c2[p][:, :]).then_inc(c2_in, 1)

        @block.vector
        def _(dve):
            done = [0]

            def link(ins):
                done[0] += 1
                ins.then_inc(link_ok, 1)
                dve.wait_ge(link_ok, done[0])

            link(dve.memset(flat(heads[:, :, :]), 0.0))
            link(dve.reciprocal(k_inv[:, :], K.context[:, :, P]))
            link(dve.tensor_scalar(k_inv[:, :], k_inv[:, :], HEAD_DIM ** -0.5, None, ALU.mult))
            for p in range(PAIRS):
                for h in range(2):
                    r = slice(h * HEAD_DIM, (h + 1) * HEAD_DIM)
                    link(dve.tensor_scalar(heads[r, p, r], K.context[r, p, r], k_inv[r, p:p + 1], None, ALU.mult))
            dve.sem_inc(heads_ok, 1)
            link(dve.tensor_scalar(K.deg[:, :], K.deg[:, :], 1.0, None, ALU.max))
            link(dve.reciprocal(K.deg[:, :], K.deg[:, :]))
            link(dve.tensor_scalar(K.run[:, :], K.pos[:, 0:EXPERTS], float(BUCKET), None, ALU.mult))
            link(dve.tensor_scalar(K.falling[:, :], K.pos[:, 0:EXPERTS], -1.0, float(EXPERTS), ALU.mult, ALU.add))
            dve.wait_ge(w_in, 32)
            dve.tensor_reduce(wmax[:, :], w32[:, :, :, :].rearrange("p a b c -> p (a b c)"), AX.X, ALU.max,
                              apply_absolute_value=True).then_inc(wmax_ok, 1)
            dve.wait_ge(wall_ok, 1)
            power_of_two(dve, link, wscale[:, :], wall[:, :], K.unscale[:, :], wbits[:, :])
            link(dve.tensor_scalar(K.unscale[:, :], K.unscale[:, :], 1.0 / XS, None, ALU.mult))
            w = w32[:, :, :, :].rearrange("p a b c -> p (a b c)")
            hi, lo = (x[:, :, :, :].rearrange("p a b c -> p (a b c)") for x in (K.wn_hi, K.wn_lo))
            link(dve.tensor_scalar(hi, w, wscale[:, :], None, ALU.mult))
            link(dve.scalar_tensor_tensor(out=lo, in0=w, scalar=wscale[:, :], in1=hi, op0=ALU.mult, op1=ALU.subtract))


def mix(nc, K, D):
    with ExitStack() as ctx:
        m = Memory(nc, ctx, "mix")
        xrow, x_t = m.sb("xrow", [P, 2 * KC, P], F16), m.sb("x_t", [P, 3, 2 * KC, P], F16)
        qrow, q_t = m.sb("qrow", [P, KC, P]), m.sb("q_t", [P, 3, KC, P])
        mean, halves = m.sb("mean", [P, DIM]), m.sb("halves", [P, 2 * KC, P], F16)
        m_t = m.sb("m_t", [P, 3, 2 * KC, P], F16)
        xres = m.sb("xres", [P, DIM])
        h, hn, hg, on = (m.sb(s, [P, DIM]) for s in ("h", "hn", "hg", "on"))
        stats, mv = m.sb("stats", [P, 2, 6]), m.sb("mv", [P, 2, 2])
        rstd, sd, shift = m.sb("rstd", [P, 2]), m.sb("sd", [P, 2]), m.sb("shift", [P, 2])
        stats1, mv1, sd1 = m.sb("stats1", [P, 6]), m.sb("mv1", [P, 2]), m.sb("sd1", [P, 1])
        x1 = m.sb("x1", [P, CHUNK, X1W])
        y, y_t = m.sb("y", [P, CHUNK, KC, P]), m.sb("y_t", [P, KC, P])
        logit, top, hot = m.sb("logit", [P, EXPERTS]), m.sb("top", [P, 1]), m.sb("hot", [P, EXPERTS])
        place, slot_f = m.sb("place", [P, EXPERTS]), m.sb("slot_f", [P, 1])
        slots, ids = m.sb("slots", [P, 1], I32), m.sb("ids", [P, 1], I32)
        tpx, tpm = m.ps("tpx", [P, 2 * KC, P], F16), m.ps("tpm", [P, 2 * KC, P], F16)
        tpq, tpy = m.ps("tpq", [P, KC, P]), m.ps("tpy", [P, KC, P])
        g, o = m.ps("g", [P, DIM]), m.ps("o", [P, DIM])
        small = m.ps("small", [P, 512])
        lg, rank, total = small[:, 0:8], small[:, 8:16], small[:, 16:24]
        S = Names()
        S.ids_st = K.ids_st
        (S.xr_in, S.q_in, S.xres_in, S.tpx_ok, S.tpq_ok, S.tpm_ok, S.x_t_ok, S.q_t_ok, S.m_t_ok, S.mean_ok,
         S.hi_ok, S.lo_ok, S.g_ok, S.o_ok, S.h_ok, S.var_ok, S.sd_ok, S.norm_ok, S.hn_ok, S.on_ok, S.sum_ok,
         S.x1_ok, S.var1_ok, S.sd1_ok, S.norm1_ok, S.y_ok, S.tpy_ok, S.y_t_ok, S.lg_ok, S.hot_ok, S.rank_ok,
         S.slot_ok, S.chain_a, S.chain_b, S.chain_c, S.chain_d, S.x1_st, S.spare, S.ids_ok) = (
            m.sem(name) for name in (
             "xr_in q_in xres_in tpx_ok tpq_ok tpm_ok x_t_ok q_t_ok m_t_ok mean_ok hi_ok lo_ok g_ok o_ok h_ok "
             "var_ok sd_ok norm_ok hn_ok on_ok sum_ok x1_ok var1_ok sd1_ok norm1_ok y_ok tpy_ok y_t_ok lg_ok "
             "hot_ok rank_ok slot_ok chain_a chain_b chain_c chain_d x1_st spare ids_ok").split())
        LAG_GO, LAG_NORM, LAG_TAIL = 1, 2, 3
        block = ctx.enter_context(nc.Block())

        def third(i):
            i %= CHUNK
            return 2 if i == CHUNK - 1 else i % 2

        @block.sync
        def _(sp):
            def load(t):
                wait_past(sp, S.tpx_ok, t)
                sp.dma_start(flat(xrow[:, :, :]), D["table"][bass.ds(t * P, P), :]).then_inc(S.xr_in, 16)
                wait_past(sp, S.tpq_ok, t)
                sp.dma_start(flat(qrow[:, :, :]), D["q"][bass.ds(t * P, P), :]).then_inc(S.q_in, 16)

            def body(t, i):
                if (a := stage(TILES, t, 0)) is not None:
                    load(a)
                if (a := stage(TILES, t, LAG_NORM)) is not None:
                    wait_past(sp, S.sum_ok, a)
                    sp.dma_start(xres[:, :], D["x"][bass.ds(a * P, P), :]).then_inc(S.xres_in, 16)
                if (a := stage(TILES, t, LAG_TAIL)) is not None:
                    sp.wait_ge(S.hot_ok, a + 1)
                    sp.dma_start(D["x1"][bass.ds(a * P, P), :], x1[:, (i - LAG_TAIL) % CHUNK, :]).then_inc(S.x1_st, 16)

            in_turn(sp, TILES, CHUNK, LAG_TAIL, body)
            sp.wait_ge(S.x1_st, 16 * TILES)

        @block.gpsimd
        def _(pool):
            def body(t, i):
                if (a := stage(TILES, t, LAG_NORM)) is not None:
                    pool.wait_ge(S.xres_in, 16 * (a + 1))
                    pool.tensor_tensor(xres[:, :], xres[:, :], K.vec[:, 2, :], ALU.add).then_inc(S.chain_c, 1)
                    pool.wait_ge(S.hn_ok, a + 1)
                    wait_past(pool, S.x1_ok, a)
                    pool.tensor_tensor(hg[:, :], hn[:, :], K.vec[:, 1, :], ALU.mult).then_inc(S.chain_c, 1)
                    pool.wait_ge(S.chain_c, 2 * a + 2)
                    pool.tensor_tensor(hg[:, :], hg[:, :], xres[:, :], ALU.add).then_inc(S.sum_ok, 1)
                if (a := stage(TILES, t, LAG_TAIL)) is not None:
                    pool.wait_ge(S.slot_ok, a + 1)
                    pool.sem_inc(S.spare, 1)
                    pool.indirect_dma_start(D["perm"], bass.IndirectOffsetOnAxis(ap=slots[:, :], axis=0),
                                            ids[:, :], None).then_inc(S.ids_st, 16)

            in_turn(pool, TILES, CHUNK, LAG_TAIL, body)
            pool.wait_ge(S.ids_st, 16 * TILES)

        @block.tensor
        def _(pe):
            def body(t, i):
                tile, go, tail = (stage(TILES, t, n) for n in (0, LAG_GO, LAG_TAIL))
                if tail is not None:
                    pe.wait_ge(S.y_ok, tail + 1)
                    wait_past(pe, S.y_t_ok, tail)
                    for k in range(KC):
                        mm = pe.transpose(tpy[:, k, :], y[:, (i - LAG_TAIL) % CHUNK, k, :], K.ident[:, :])
                    mm.then_inc(S.tpy_ok, 1)
                if tile is not None:
                    pe.wait_ge(S.xr_in, 16 * (tile + 1))
                    wait_past(pe, S.x_t_ok, tile)
                    for k in range(2 * KC):
                        mm = pe.transpose(tpx[:, k, :], xrow[:, k, :], K.ident16[:, :])
                    mm.then_inc(S.tpx_ok, 1)
                    pe.wait_ge(S.q_in, 16 * (tile + 1))
                    wait_past(pe, S.q_t_ok, tile)
                    for k in range(KC):
                        mm = pe.transpose(tpq[:, k, :], qrow[:, k, :], K.ident[:, :])
                    mm.then_inc(S.tpq_ok, 1)
                if tail is not None:
                    pe.wait_ge(S.y_t_ok, tail + 1)
                    wait_past(pe, S.slot_ok, tail)
                    for k in range(KC):
                        mm = pe.matmul(lg, y_t[:, k, :], K.wg[:, k, :], start=(k == 0), stop=(k == KC - 1))
                    mm.then_inc(S.lg_ok, 1)
                if go is not None:
                    b = third(i - LAG_GO)
                    pe.wait_ge(S.x_t_ok, go + 1)
                    pe.wait_ge(S.m_t_ok, go + 1)
                    wait_past(pe, S.h_ok, go)
                    todo = [(src, w, a, half, k) for src, w in ((x_t, 0), (m_t, 1)) for k in range(KC)
                            for a, half in ((0, K.wn_hi), (0, K.wn_lo), (KC, K.wn_hi))]
                    for j, (src, w, a, half, k) in enumerate(todo):
                        mm = pe.matmul(g[:, :], src[:, b, a + k, :], half[:, w, k, :], start=(j == 0),
                                       stop=(j == len(todo) - 1))
                    mm.then_inc(S.g_ok, 1)
                if tile is not None:
                    pe.wait_ge(S.lo_ok, tile + 1)
                    wait_past(pe, S.m_t_ok, tile)
                    for k in range(2 * KC):
                        mm = pe.transpose(tpm[:, k, :], halves[:, k, :], K.ident16[:, :])
                    mm.then_inc(S.tpm_ok, 1)
                if tail is not None:
                    pe.wait_ge(S.hot_ok, tail + 1)
                    pe.matmul(rank, K.upper[:, :], hot[:, :], start=True, stop=True)
                    pe.matmul(total, K.ones[:, :], hot[:, :], start=True, stop=True).then_inc(S.rank_ok, 1)
                if go is not None:
                    pe.wait_ge(S.q_t_ok, go + 1)
                    wait_past(pe, S.on_ok, go)
                    for k in range(KC):
                        mm = pe.matmul(o[:, :], q_t[:, b, k, :], K.c2[:, k, :], start=(k == 0), stop=(k == KC - 1))
                    mm.then_inc(S.o_ok, 1)

            in_turn(pe, TILES, CHUNK, LAG_TAIL, body)

        @block.scalar
        def _(act):
            def body(t, i):
                tile, norm, tail = (stage(TILES, t, n) for n in (0, LAG_NORM, LAG_TAIL))
                if tail is not None:
                    act.wait_ge(S.tpy_ok, tail + 1)
                    wait_past(act, S.lg_ok, tail)
                    act.copy(y_t[:, :, :], tpy[:, :, :]).then_inc(S.y_t_ok, 1)
                if tile is not None:
                    act.wait_ge(S.tpx_ok, tile + 1)
                    wait_past(act, S.g_ok, tile - 1)
                    act.copy(x_t[:, third(i), :, :], tpx[:, :, :]).then_inc(S.x_t_ok, 1)
                    act.wait_ge(S.tpq_ok, tile + 1)
                    wait_past(act, S.o_ok, tile - 1)
                    act.copy(q_t[:, third(i), :, :], tpq[:, :, :]).then_inc(S.q_t_ok, 1)
                if norm is not None:
                    n = (i - LAG_NORM) % CHUNK
                    act.wait_ge(S.var_ok, norm + 1)
                    act.activation(sd[:, :], rstd[:, :], ACT.Sqrt).then_inc(S.sd_ok, 1)
                    act.wait_ge(S.norm_ok, norm + 1)
                    wait_past(act, S.sum_ok, norm)
                    act.activation(hn[:, :], h[:, :], ACT.Identity, bias=shift[:, 0:1], scale=rstd[:, 0:1]).then_inc(S.hn_ok, 1)
                    act.activation(on[:, :], o[:, :], ACT.Identity, bias=shift[:, 1:2], scale=rstd[:, 1:2]).then_inc(S.on_ok, 1)
                if tile is not None:
                    act.wait_ge(S.mean_ok, tile + 1)
                    wait_past(act, S.tpm_ok, tile)
                    act.copy(flat(halves[:, 0:KC, :]), mean[:, :]).then_inc(S.hi_ok, 1)
                if norm is not None:
                    act.wait_ge(S.var1_ok, norm + 1)
                    act.activation(sd1[:, :], x1[:, n, DIM:DIM + 1], ACT.Sqrt).then_inc(S.sd1_ok, 1)
                    act.wait_ge(S.norm1_ok, norm + 1)
                    act.activation(y[:, n, :, :].rearrange("p a b -> p (a b)"), x1[:, n, 0:DIM], ACT.Identity,
                                   bias=x1[:, n, DIM + 1:DIM + 2], scale=x1[:, n, DIM:DIM + 1]).then_inc(S.y_ok, 1)
                if tile is not None:
                    act.wait_ge(S.tpm_ok, tile + 1)
                    wait_past(act, S.g_ok, tile - 1)
                    act.copy(m_t[:, third(i), :, :], tpm[:, :, :]).then_inc(S.m_t_ok, 1)

            in_turn(act, TILES, CHUNK, LAG_TAIL, body)

        @block.vector
        def _(dve):
            dve.memset(x1[:, :, DIM:X1W], 0.0).then_inc(S.ids_ok, 1)
            dve.tensor_copy(ids[:, :], K.node[:, :]).then_inc(S.ids_ok, 1)
            dve.wait_ge(S.ids_ok, 2)

            def body(t, i):
                tile, norm, tail = (stage(TILES, t, n) for n in (0, LAG_NORM, LAG_TAIL))
                if norm is not None:
                    n = (i - LAG_NORM) % CHUNK
                    step = Chain(dve, S.chain_a, 8, norm)
                    dve.wait_ge(S.g_ok, norm + 1)
                    dve.scalar_tensor_tensor(out=h[:, :], in0=g[:, :], scalar=K.unscale[:, :], in1=K.vec[:, 0, :],
                                             op0=ALU.mult, op1=ALU.add).then_inc(S.h_ok, 1)
                    dve.wait_ge(S.h_ok, norm + 1)
                    dve.bn_stats(stats[:, 0, :], h[:, :])
                    dve.wait_ge(S.o_ok, norm + 1)
                    step(dve.bn_stats(stats[:, 1, :], o[:, :]))
                    dve.sem_inc(S.spare, 1)
                    dve.bn_aggr(mv[:, 0, :], stats[:, 0, :])
                    step(dve.bn_aggr(mv[:, 1, :], stats[:, 1, :]))
                    dve.tensor_scalar(rstd[:, :], mv[:, :, 1], EPS, None, ALU.add).then_inc(S.var_ok, 1)
                if tile is not None:
                    wait_past(dve, S.lo_ok, tile)
                    wait_past(dve, S.hi_ok, tile)
                    dve.tensor_scalar(mean[:, :], flat(K.acc[:, bass.ds(tile, 1), :]), K.deg[:, bass.ds(tile, 1)], None,
                                      ALU.mult).then_inc(S.mean_ok, 1)
                if norm is not None:
                    dve.wait_ge(S.sd_ok, norm + 1)
                    step(dve.reciprocal(rstd[:, :], sd[:, :]))
                    step(dve.tensor_tensor(shift[:, :], mv[:, :, 0], rstd[:, :], ALU.mult))
                    dve.tensor_scalar(shift[:, :], shift[:, :], -1.0, None, ALU.mult).then_inc(S.norm_ok, 1)
                if tail is not None:
                    link = Chain(dve, S.chain_b, 4, tail)
                    rest = x1[:, (i - LAG_TAIL) % CHUNK, DIM + 2:DIM + 2 + EXPERTS]
                    dve.wait_ge(S.lg_ok, tail + 1)
                    link(dve.tensor_tensor(logit[:, :], lg, K.bg[:, :], ALU.add))
                    link(dve.tensor_reduce(top[:, :], logit[:, :], AX.X, ALU.max))
                    dve.tensor_scalar(rest, logit[:, :], top[:, :], None, ALU.subtract)
                    link(dve.scalar_tensor_tensor(out=logit[:, :], in0=logit[:, :], scalar=top[:, :],
                                                  in1=K.falling[:, :], op0=ALU.is_equal, op1=ALU.mult))
                    link(dve.tensor_reduce(top[:, :], logit[:, :], AX.X, ALU.max))
                    dve.tensor_scalar(hot[:, :], logit[:, :], top[:, :], None, ALU.is_equal).then_inc(S.hot_ok, 1)
                if norm is not None:
                    wait_past(dve, S.x1_st, 16 * (norm - CHUNK + 3))
                    dve.wait_ge(S.on_ok, norm + 1)
                    step(dve.tensor_tensor(on[:, :], on[:, :], K.vec[:, 3, :], ALU.mult))
                if tile is not None:
                    dve.wait_ge(S.hi_ok, tile + 1)
                    dve.tensor_tensor(flat(halves[:, KC:, :]), mean[:, :], flat(halves[:, 0:KC, :]),
                                      ALU.subtract).then_inc(S.lo_ok, 1)
                if norm is not None:
                    dve.wait_ge(S.sum_ok, norm + 1)
                    dve.tensor_tensor(x1[:, n, 0:DIM], on[:, :], hg[:, :], ALU.add).then_inc(S.x1_ok, 1)
                    dve.wait_ge(S.x1_ok, norm + 1)
                    step(dve.bn_stats(stats1[:, :], x1[:, n, 0:DIM]))
                    dve.sem_inc(S.spare, 1)
                    step(dve.bn_aggr(mv1[:, :], stats1[:, :]))
                    dve.tensor_scalar(x1[:, n, DIM:DIM + 1], mv1[:, 1:2], EPS, None, ALU.add).then_inc(S.var1_ok, 1)
                    dve.wait_ge(S.sd1_ok, norm + 1)
                    step(dve.reciprocal(x1[:, n, DIM:DIM + 1], sd1[:, :]))
                    dve.scalar_tensor_tensor(out=x1[:, n, DIM + 1:DIM + 2], in0=mv1[:, 0:1], scalar=-1.0,
                                             in1=x1[:, n, DIM:DIM + 1], op0=ALU.mult, op1=ALU.mult).then_inc(S.norm1_ok, 1)
                if tail is not None:
                    link = Chain(dve, S.chain_d, 4, tail)
                    dve.wait_ge(S.rank_ok, tail + 1)
                    wait_past(dve, S.ids_st, 16 * tail)
                    link(dve.tensor_tensor(place[:, :], K.run[:, :], rank, ALU.add))
                    link(dve.tensor_tensor(place[:, :], place[:, :], hot[:, :], ALU.mult))
                    link(dve.tensor_reduce(slot_f[:, :], place[:, :], AX.X, ALU.add))
                    dve.tensor_copy(slots[:, :], slot_f[:, :])
                    dve.tensor_scalar(ids[:, :], K.node[:, :], 0.0, None, ALU.add)
                    link(dve.tensor_scalar(K.node[:, :], K.node[:, :], float(P), None, ALU.add))
                    dve.tensor_tensor(K.run[:, :], K.run[:, :], total, ALU.add).then_inc(S.slot_ok, 1)
                    dve.wait_ge(S.slot_ok, tail + 1)

            in_turn(dve, TILES, CHUNK, LAG_TAIL, body)


def experts(nc, K, D):
    U = UNROLL
    LAG_Y, LAG_TY, LAG_H, LAG_TH, LAG_F = range(5)
    with ExitStack() as ctx:
        m = Memory(nc, ctx, "experts")
        w1, w2 = m.sb("w1", [P, EXPERTS, KC, HIDDEN]), m.sb("w2", [P, EXPERTS, 2, DIM])
        b1, b2 = m.sb("b1", [P, 2, EXPERTS]), m.sb("b2", [P, EXPERTS, DIM])
        e_row, e_int = m.sb("e_row", [1, 6, EXPERTS]), m.sb("e_int", [1, EXPERTS], I32)
        t_in, t_val = m.sb("t_in", [1, XT, EXPERTS]), m.sb("t_val", [1, 2, XT, EXPERTS])
        t_sum = m.sb("t_sum", [1, 3, XT])
        lots = m.sb("lots", [1, 2, XT], I32)
        idx = m.sb("idx", [P, U], I32)
        rows, out = m.sb("rows", [P, U, X1W]), m.sb("out", [P, U, DIM])
        y, y_t = m.sb("y", [P, 2, KC, P]), m.sb("y_t", [P, 2, KC, P])
        h, h_t, f = m.sb("h", [P, 2, HIDDEN]), m.sb("h_t", [P, 2, 2, P]), m.sb("f", [P, DIM])
        ex, score = m.sb("ex", [P, EXPERTS]), m.sb("score", [P, U])
        tpy = [m.ps(f"tpy{i}", [P, KC, P]) for i in range(2)]
        hp = [m.ps(f"hp{i}", [P, HIDDEN]) for i in range(2)]
        tph = [m.ps(f"tph{i}", [P, 2, P]) for i in range(2)]
        fp = [m.ps(f"fp{i}", [P, DIM]) for i in range(2)]
        S = Names()
        (S.w1_in, S.w2_in, S.b1_in, S.b2_in, S.link_ok, S.lots_ok, S.cleared, S.y_ok, S.sum_ok, S.score_ok, S.tpy_ok, S.y_t_ok,
         S.hp_ok, S.h_ok, S.tph_ok, S.h_t_ok, S.fp_ok, S.f_ok, S.out_ok, S.spare, S.slot_seen) = (
            m.sem(name) for name in (
             "w1_in w2_in b1_in b2_in link_ok lots_ok cleared y_ok sum_ok score_ok tpy_ok y_t_ok hp_ok h_ok tph_ok h_t_ok "
             "fp_ok f_ok out_ok spare slot_seen").split())
        idx_in, rows_in, out_st = m.sems("idx_in", U), K.rows_in, K.out_st
        block = ctx.enter_context(nc.Block())

        def turns(t, i):
            return t // U + 1 if isinstance(t, int) else (t - i) // U + 1

        @block.sync
        def _(sp):
            sp.dma_start(b1[:, :, :], D["b1"]).then_inc(S.b1_in, 16)
            sp.dma_start(w1[:, :, :, :], D["w1"]).then_inc(S.w1_in, 16)
            sp.wait_ge(S.lots_ok, 1)

            def round_(c):
                for i in range(U):
                    t = U * c + i
                    at = sp.value_load(lots[0:1, 1, bass.ds(t, 1)], min_val=0, max_val=EXPERTS * BUCKET)
                    wait_past(sp, out_st[i], 16 * c)
                    sp.sem_inc(S.slot_seen, 1)
                    sp.dma_start(idx[:, i:i + 1], D["perm"][bass.ds(at, P), :]).then_inc(idx_in[i], 16)

            round_(0)
            sp.dma_start(w2[:, :, :, :], D["w2"]).then_inc(S.w2_in, 16)
            sp.dma_start(flat(b2[:, :, :]), D["b2"].to_broadcast([P, EXPERTS * DIM])).then_inc(S.b2_in, 16)
            with sp.Fori(1, XT // U) as c:
                round_(c)

        @block.gpsimd
        def _(pool):
            pool.memset(rows[:, :, :], 0.0).then_inc(S.cleared, 1)
            pool.wait_ge(S.cleared, 1)

            def round_(c):
                for i in range(U):
                    pool.wait_ge(idx_in[i], 16 * (c + 1))
                    pool.sem_inc(S.spare, 1)
                    pool.indirect_dma_start(rows[:, i, :], None, D["x1"],
                                            bass.IndirectOffsetOnAxis(ap=idx[:, i:i + 1], axis=0),
                                            bounds_check=ROWS - 1, oob_is_err=False).then_inc(rows_in[i], 16)
                    j = (i - 5) % U
                    if i < 5 and isinstance(c, int) and c == 0:
                        continue
                    scatter(U * c + i - 5, j)

            def scatter(t, j):
                pool.wait_ge(S.out_ok, t + 1)
                pool.sem_inc(S.spare, 1)
                pool.indirect_dma_start(D["out"], bass.IndirectOffsetOnAxis(ap=idx[:, j:j + 1], axis=0), out[:, j, :],
                                        None, bounds_check=ROWS - 1, oob_is_err=False).then_inc(out_st[j], 16)

            round_(0)
            with pool.Fori(1, XT // U) as c:
                round_(c)
            for t in range(XT - 5, XT):
                scatter(t, t % U)
            for i in range(U):
                pool.wait_ge(out_st[i], 16 * (XT // U))

        @block.tensor
        def _(pe):
            def body(t, i):
                if (a := stage(XT, t, LAG_TY)) is not None:
                    b = (i - LAG_TY) % 2
                    pe.wait_ge(S.y_ok, a + 1)
                    wait_past(pe, S.y_t_ok, a - 1)
                    for k in range(KC):
                        mm = pe.transpose(tpy[b][:, k, :], y[:, b, k, :], K.ident[:, :])
                    mm.then_inc(S.tpy_ok, 1)
                if (a := stage(XT, t, LAG_H)) is not None:
                    b = (i - LAG_H) % 2
                    e = pe.value_load(lots[0:1, 0, bass.ds(a, 1)], min_val=0, max_val=EXPERTS - 1)
                    pe.wait_ge(S.y_t_ok, a + 1)
                    wait_past(pe, S.h_ok, a - 1)
                    for k in range(KC):
                        mm = pe.matmul(hp[b][:, :], y_t[:, b, k, :], flat(w1[:, bass.ds(e, 1), k, :]), start=(k == 0),
                                       stop=(k == KC - 1))
                    mm.then_inc(S.hp_ok, 1)
                if (a := stage(XT, t, LAG_TH)) is not None:
                    b = (i - LAG_TH) % 2
                    pe.wait_ge(S.h_ok, a + 1)
                    wait_past(pe, S.h_t_ok, a - 1)
                    for k in range(2):
                        mm = pe.transpose(tph[b][:, k, :], h[:, b, k * P:(k + 1) * P], K.ident[:, :])
                    mm.then_inc(S.tph_ok, 1)
                if (a := stage(XT, t, LAG_F)) is not None:
                    b = (i - LAG_F) % 2
                    e = pe.value_load(lots[0:1, 0, bass.ds(a, 1)], min_val=0, max_val=EXPERTS - 1)
                    pe.wait_ge(S.h_t_ok, a + 1)
                    wait_past(pe, S.f_ok, a - 1)
                    if isinstance(a, int) and a == 0:
                        pe.wait_ge(S.w2_in, 16)
                    for k in range(2):
                        mm = pe.matmul(fp[b][:, :], h_t[:, b, k, :], flat(w2[:, bass.ds(e, 1), k, :]), start=(k == 0),
                                       stop=(k == 1))
                    mm.then_inc(S.fp_ok, 1)

            pe.wait_ge(S.w1_in, 16)
            pe.wait_ge(S.lots_ok, 1)
            in_turn(pe, XT, U, LAG_F, body)

        @block.scalar
        def _(act):
            def body(t, i):
                if (a := stage(XT, t, LAG_TY)) is not None:
                    b = (i - LAG_TY) % 2
                    act.wait_ge(S.tpy_ok, a + 1)
                    wait_past(act, S.hp_ok, a - 1)
                    act.copy(y_t[:, b, :, :], tpy[b][:, :, :]).then_inc(S.y_t_ok, 1)
                if (a := stage(XT, t, LAG_H)) is not None:
                    b = (i - LAG_H) % 2
                    act.wait_ge(S.hp_ok, a + 1)
                    wait_past(act, S.tph_ok, a - 1)
                    act.copy(h[:, b, :], hp[b][:, :]).then_inc(S.h_ok, 1)
                if (a := stage(XT, t, LAG_Y)) is not None:
                    act.wait_ge(rows_in[i], 16 * turns(a, i))
                    wait_past(act, S.tpy_ok, a - 1)
                    act.activation(y[:, i % 2, :, :].rearrange("p a b -> p (a b)"), rows[:, i, 0:DIM], ACT.Identity,
                                   bias=rows[:, i, DIM + 1:DIM + 2], scale=rows[:, i, DIM:DIM + 1]).then_inc(S.y_ok, 1)
                    wait_past(act, S.score_ok, a)
                    act.activation(ex[:, :], rows[:, i, DIM + 2:DIM + 2 + EXPERTS], ACT.Exp,
                                   accum_out=score[:, i:i + 1]).then_inc(S.sum_ok, 1)

            in_turn(act, XT, U, LAG_F, body)

        @block.vector
        def _(dve):
            done = [0]

            def link(ins):
                done[0] += 1
                ins.then_inc(S.link_ok, 1)
                dve.wait_ge(S.link_ok, done[0])

            count, tiles, first, after, value, e_num = (e_row[:, k, :] for k in range(6))
            link(dve.tensor_copy(e_num, K.pos[0:1, 0:EXPERTS]))
            link(dve.tensor_scalar(value, e_num, float(-BUCKET), None, ALU.mult))
            link(dve.tensor_tensor(count, K.run[0:1, :], value, ALU.add))
            link(dve.tensor_scalar(e_int[:, :], count, float(P - 1), None, ALU.add))
            link(dve.tensor_scalar(e_int[:, :], e_int[:, :], 7, None, ALU.arith_shift_right))
            link(dve.tensor_copy(tiles, e_int[:, :]))
            link(dve.memset(first, 0.0))
            for e in range(1, EXPERTS):
                link(dve.tensor_tensor(first[:, e:e + 1], first[:, e - 1:e], tiles[:, e - 1:e], ALU.add))
            link(dve.tensor_tensor(after, first, tiles, ALU.add))
            num = bcast(K.pos[0:1, 0:XT], EXPERTS)

            def all_tiles(v):
                return v.unsqueeze(1).to_broadcast([1, XT, EXPERTS])

            link(dve.tensor_tensor(t_in[:, :, :], num, all_tiles(first), ALU.is_ge))
            link(dve.tensor_tensor(t_val[:, 0, :, :], num, all_tiles(after), ALU.is_lt))
            link(dve.tensor_tensor(t_in[:, :, :], t_in[:, :, :], t_val[:, 0, :, :], ALU.mult))
            link(dve.tensor_scalar(count, first, float(-P), float(-EXPERTS * BUCKET), ALU.mult, ALU.add))
            link(dve.tensor_tensor(count, count, value, ALU.subtract))
            link(dve.tensor_tensor(t_val[:, 0, :, :], t_in[:, :, :], all_tiles(e_num), ALU.mult))
            link(dve.tensor_tensor(t_val[:, 1, :, :], t_in[:, :, :], all_tiles(count), ALU.mult))
            link(dve.tensor_reduce(t_sum[:, 0, :], t_in[:, :, :], AX.X, ALU.add))
            link(dve.tensor_reduce(t_sum[:, 1, :], t_val[:, 1, :, :], AX.X, ALU.add))
            link(dve.tensor_reduce(t_sum[:, 2, :], t_val[:, 0, :, :], AX.X, ALU.add))
            link(dve.tensor_tensor(t_sum[:, 0, :], t_sum[:, 0, :], K.pos[0:1, 0:XT], ALU.mult))
            link(dve.tensor_scalar(t_sum[:, 0, :], t_sum[:, 0, :], float(P), float(EXPERTS * BUCKET), ALU.mult, ALU.add))
            link(dve.tensor_tensor(lots[:, 1, :], t_sum[:, 0, :], t_sum[:, 1, :], ALU.add))
            dve.tensor_copy(lots[:, 0, :], t_sum[:, 2, :]).then_inc(S.lots_ok, 1)
            dve.wait_ge(S.lots_ok, 1)
            dve.wait_ge(S.b1_in, 16)

            def body(t, i):
                if (a := stage(XT, t, LAG_Y)) is not None:
                    dve.wait_ge(S.sum_ok, a + 1)
                    dve.reciprocal(score[:, i:i + 1], score[:, i:i + 1]).then_inc(S.score_ok, 1)
                if (a := stage(XT, t, LAG_TH)) is not None:
                    b = (i - LAG_TH) % 2
                    e = dve.value_load(lots[0:1, 0, bass.ds(a, 1)], min_val=0, max_val=EXPERTS - 1)
                    dve.wait_ge(S.tph_ok, a + 1)
                    wait_past(dve, S.fp_ok, a - 1)
                    for k in range(2):
                        ins = dve.tensor_scalar(h_t[:, b, k, :], tph[b][:, k, :], b1[:, k, bass.ds(e, 1)], 0.0,
                                                ALU.add, ALU.max)
                    ins.then_inc(S.h_t_ok, 1)
                if (a := stage(XT, t, LAG_F)) is not None:
                    b, j = (i - LAG_F) % 2, (i - LAG_F) % U
                    e = dve.value_load(lots[0:1, 0, bass.ds(a, 1)], min_val=0, max_val=EXPERTS - 1)
                    dve.wait_ge(S.fp_ok, a + 1)
                    wait_past(dve, S.out_ok, a)
                    if isinstance(a, int) and a == 0:
                        dve.wait_ge(S.b2_in, 16)
                    dve.tensor_tensor(f[:, :], fp[b][:, :], flat(b2[:, bass.ds(e, 1), :]), ALU.add).then_inc(S.f_ok, 1)
                    dve.wait_ge(S.f_ok, a + 1)
                    if not (isinstance(a, int) and a < U):
                        dve.wait_ge(out_st[j], 16 * (turns(a, j) - 1))
                    dve.scalar_tensor_tensor(out=out[:, j, :], in0=f[:, :], scalar=score[:, j:j + 1],
                                             in1=rows[:, j, 0:DIM], op0=ALU.mult, op1=ALU.add).then_inc(S.out_ok, 1)

            in_turn(dve, XT, U, LAG_F, body)


def program(nc, D):
    with ExitStack() as ctx:
        m = Memory(nc, ctx, "all")
        K = Names()
        K.g_in = m.sems("g_in", RING)
        K.ids_st = m.sem("ids_st")
        K.rows_in = m.sems("rows_in", UNROLL)
        K.out_st = m.sems("out_st", UNROLL)
        K.ident = m.sb("ident", [P, P])
        K.upper = m.sb("upper", [P, P])
        K.ones = m.sb("ones", [P, P])
        K.ident16 = m.sb("ident16", [P, P], F16)
        K.iota16 = m.sb("iota16", [P, P], F16)
        K.ones16 = m.sb("ones16", [P, 1], F16)
        K.pos = m.sb("pos", [P, 512])
        K.pad_bias = m.sb("pad_bias", [P, TILES])
        K.rq = m.sb("rq", [P, TILES])
        K.deg = m.sb("deg", [P, TILES])
        K.context = m.sb("context", [P, PAIRS, P + 1])
        K.m_old = m.sb("m_old", [P, PAIRS])
        K.run = m.sb("run", [P, EXPERTS])
        K.node = m.sb("node", [P, 1])
        K.scratch = m.sb("scratch", [P, 64])
        acc_held = ctx.enter_context(ExitStack())
        K.acc = Memory(nc, acc_held, "held").sb("acc", [P, TILES, DIM])
        with ExitStack() as early:
            m2 = Memory(nc, early, "early")
            K.rel = m2.sb("rel", [P, GROUP, ENTRIES + AHEAD])
            K.idx = m2.sb("idx", [P, ENTRIES, GROUP], I32)
            K.packs = m2.sb("packs", [1, ENTRIES // PACK], I32)
            K.rounds = m2.sb("rounds", [1, 1], I32)
            K.gfirst, K.gstart, K.gend = (m2.sb(n, [G_PART, G_BLOCKS]) for n in ("gfirst", "gstart", "gend"))
            K.kmax = m2.sb("kmax", [P, DIM])
            K.wq_hi, K.wq_lo = m2.sb("wq_hi", [P, KC, 3 * DIM], F16), m2.sb("wq_lo", [P, KC, 3 * DIM], F16)
            normalize(nc, K, D)
            aggregate(nc, K, D)
            further = nc.values_load(K.rounds[0:1, 0:1], min_val=0, max_val=ROUNDS)
            with nc.If(further > 0):
                with nc.Fori(0, further):
                    next_round(nc, K, D)
            nc.all_engine_barrier()
        with ExitStack() as late:
            m2 = Memory(nc, late, "late")
            K.wn_hi, K.wn_lo = m2.sb("wn_hi", [P, 2, KC, DIM], F16), m2.sb("wn_lo", [P, 2, KC, DIM], F16)
            K.c2, K.vec = m2.sb("c2", [P, PAIRS, DIM]), m2.sb("vec", [P, 4, DIM])
            K.wg, K.bg, K.falling = m2.sb("wg", [P, KC, EXPERTS]), m2.sb("bg", [P, EXPERTS]), m2.sb("falling", [P, EXPERTS])
            K.unscale = m2.sb("unscale", [P, 1])
            fold(nc, K, D)
            mix(nc, K, D)
        acc_held.close()
        experts(nc, K, D)


def lay_out(a):
    def rows(w):
        return np.ascontiguousarray(w.reshape(-1, P, w.shape[-1]).transpose(1, 0, 2))

    x = np.zeros((ROWS, DIM), np.float32)
    x[:N_NODES] = a["x"]
    src = np.zeros(GROUPS * GROUP * P, np.int32)
    src[:N_EDGES] = a["src"]
    dst = np.full(GROUPS * GROUP * P, ROWS - 1, np.int32)
    dst[:N_EDGES] = a["dst"]

    def by_group(v):
        return np.ascontiguousarray(v.reshape(G_BLOCKS, G_PART, GROUP * P).transpose(1, 0, 2))

    return {
        "x": x,
        "src": by_group(src),
        "dst": by_group(dst),
        "wqkv": rows(a["L0_mix_w_qkv"].T),
        "w_self": rows(a["L0_gnn_W_self"].T),
        "w_neigh": rows(a["L0_gnn_W_neigh"].T),
        "w_out": rows(a["L0_mix_w_out"].T),
        "bias": a["L0_gnn_bias"].reshape(1, -1),
        "gamma": a["L0_gnn_gamma"].reshape(1, -1),
        "beta": a["L0_gnn_beta"].reshape(1, -1),
        "out_gamma": a["L0_mix_out_gamma"].reshape(1, -1),
        "w_gate": rows(a["L0_ffn_Wg"]),
        "b_gate": a["L0_ffn_bg"].reshape(1, -1),
        "w1": np.ascontiguousarray(a["L0_ffn_W1"].reshape(EXPERTS, KC, P, HIDDEN).transpose(2, 0, 1, 3)),
        "w2": np.ascontiguousarray(a["L0_ffn_W2"].reshape(EXPERTS, 2, P, DIM).transpose(2, 0, 1, 3)),
        "b1": np.ascontiguousarray(a["L0_ffn_b1"].reshape(EXPERTS, 2, P).transpose(2, 1, 0)),
        "b2": a["L0_ffn_b2"].reshape(1, -1),
        "norm_gamma": np.ascontiguousarray(a["L0_mix_norm_gamma"].reshape(KC, P).T),
    }


def kernel(**inputs):
    import concourse.bacc as bacc
    from concourse.bass_utils import run_bass_kernel_spmd as run

    arrays = lay_out({k: np.asarray(v) for k, v in inputs.items()})
    nc = bacc.Bacc("TRN2", target_bir_lowering=False, num_devices=1)
    D = {k: nc.dram_tensor(f"in_{k}", v.shape, mybir.dt.from_np(v.dtype), kind="ExternalInput").ap()
         for k, v in arrays.items()}
    for k, s, d in (("table", (ROWS, 2 * DIM), F16), ("q", (ROWS, DIM), F32), ("perm", (EXPERTS * BUCKET + P, 1), I32),
                    ("x1", (ROWS, X1W), F32)):
        D[k] = nc.dram_tensor(f"dram_{k}", s, d, kind="Internal").ap()
    D["out"] = nc.dram_tensor("out", (ROWS, DIM), F32, kind="ExternalOutput").ap()
    program(nc, D)
    r = run(nc, [{f"in_{k}": v for k, v in arrays.items()}], core_ids=[0])
    return r.results[0]["out"][:N_NODES]
```
